# Optimizing a Trainium2 kernel written in Bass

```python
import numpy as np
import jax
import jax.numpy as jnp

def _softmax(x, axis=-1):
    return jax.nn.softmax(x, axis=axis)

def _gelu(x):
    return jax.nn.gelu(x, approximate=True)

def _silu(x):
    return jax.nn.silu(x)

def _sigmoid(x):
    return jax.nn.sigmoid(x)

def _layernorm(x, axis=-1, eps=1e-05):
    m = jnp.mean(x, axis=axis, keepdims=True)
    v = jnp.var(x, axis=axis, keepdims=True)
    return (x - m) / jnp.sqrt(v + eps)

def _scatter_add(tgt, idx, src, axis=0):
    return tgt.at[idx].add(src)

def _segment_sum(src, seg, n):
    return jax.ops.segment_sum(src, seg, n)
kernel_name = 'mk_gnn_preln_d1_gnn_r64_127d04'

def setup_inputs(seed: int=0):
    np.random.seed(seed)
    _w = jnp.asarray

    def _rec_inputs():
        import jax
        import jax.numpy as jnp
        _gk = jax.random.key(seed)
        x = -0.000202 + 1 * jax.random.normal(jax.random.fold_in(_gk, 1), (100000, 128), jnp.float32)
        src = jax.random.randint(jax.random.fold_in(_gk, 2), (25000,), 0, 100000, jnp.int32)
        dst = jax.random.randint(jax.random.fold_in(_gk, 3), (25000,), 0, 100000, jnp.int32)
        _o = jnp.argsort(dst, stable=True)
        src = src[_o]
        dst = dst[_o]
        edge_weight = jax.random.uniform(jax.random.fold_in(_gk, 12), (25000,), jnp.float32, 0.0, 0.999998)
        return (x, src, dst, edge_weight)
    x, src, dst, edge_weight = _rec_inputs()

    def _L0_gnn_setup():
        import jax, jax.numpy as jnp
        import numpy as np
        N_NODES = 50000
        N_EDGES = 12500
        C_IN, H1, H2 = (128, 256, 128)
        EPS = 1e-05

        def _bn(x, g, b):
            m = jnp.mean(x, axis=0)
            v = jnp.var(x, axis=0)
            return g * (x - m) * jax.lax.rsqrt(v + EPS) + b

        def _gcn_conv(x, src, dst, ew, W, b, n):
            xw = x @ W
            deg = jax.ops.segment_sum(ew, dst, num_segments=n) + 1.0
            dinv = jax.lax.rsqrt(deg)
            norm = dinv[src] * ew * dinv[dst]
            agg = jax.ops.segment_sum(norm[:, None] * xw[src], dst, num_segments=n)
            return agg + xw / deg[:, None] + b

        def _graph_conv(x, src, dst, ew, Wrel, brel, Wroot, n):
            agg = jax.ops.segment_sum(ew[:, None] * x[src], dst, num_segments=n)
            return agg @ Wrel + brel + x @ Wroot
        key = jax.random.key(seed)
        ks = jax.random.split(key, 16)

        def glorot(k, shape):
            lim = float(np.sqrt(6.0 / (shape[0] + shape[1])))
            return jax.random.uniform(k, shape, jnp.float32, -lim, lim)
        return {'x': jax.random.normal(ks[0], (N_NODES, C_IN), jnp.float32), 'edge_index': jax.random.randint(ks[1], (2, N_EDGES), 0, N_NODES, jnp.int64), 'edge_weight': jax.random.uniform(ks[2], (N_EDGES,), jnp.float32), 'W1': glorot(ks[3], (C_IN, H1)), 'b1': jnp.zeros((H1,), jnp.float32), 'Wrel2': glorot(ks[4], (H1, H1)), 'brel2': jnp.zeros((H1,), jnp.float32), 'Wroot2': glorot(ks[5], (H1, H1)), 'Wrel3': glorot(ks[6], (H1, H2)), 'brel3': jnp.zeros((H2,), jnp.float32), 'Wroot3': glorot(ks[7], (H1, H2)), 'g0': jnp.ones((C_IN,), jnp.float32), 'be0': jnp.zeros((C_IN,), jnp.float32), 'g1': jnp.ones((H1,), jnp.float32), 'be1': jnp.zeros((H1,), jnp.float32), 'g2': jnp.ones((H1,), jnp.float32), 'be2': jnp.zeros((H1,), jnp.float32), 'g3': jnp.ones((H2,), jnp.float32), 'be3': jnp.zeros((H2,), jnp.float32)}
    _L0_gnn_all = _L0_gnn_setup()
    _L0_gnn_in = {k: v for k, v in _L0_gnn_all.items() if k in ('W1', 'b1', 'Wrel2', 'brel2', 'Wroot2', 'Wrel3', 'brel3', 'Wroot3', 'g0', 'be0', 'g1', 'be1', 'g2', 'be2', 'g3', 'be3')}
    del _L0_gnn_all
    return {'x': x, 'src': src, 'dst': dst, 'edge_weight': edge_weight, 'L0_gnn_W1': _L0_gnn_in['W1'], 'L0_gnn_b1': _L0_gnn_in['b1'], 'L0_gnn_Wrel2': _L0_gnn_in['Wrel2'], 'L0_gnn_brel2': _L0_gnn_in['brel2'], 'L0_gnn_Wroot2': _L0_gnn_in['Wroot2'], 'L0_gnn_Wrel3': _L0_gnn_in['Wrel3'], 'L0_gnn_brel3': _L0_gnn_in['brel3'], 'L0_gnn_Wroot3': _L0_gnn_in['Wroot3'], 'L0_gnn_g0': _L0_gnn_in['g0'], 'L0_gnn_be0': _L0_gnn_in['be0'], 'L0_gnn_g1': _L0_gnn_in['g1'], 'L0_gnn_be1': _L0_gnn_in['be1'], 'L0_gnn_g2': _L0_gnn_in['g2'], 'L0_gnn_be2': _L0_gnn_in['be2'], 'L0_gnn_g3': _L0_gnn_in['g3'], 'L0_gnn_be3': _L0_gnn_in['be3']}

def reference(x, src, dst, edge_weight, L0_gnn_W1, L0_gnn_b1, L0_gnn_Wrel2, L0_gnn_brel2, L0_gnn_Wroot2, L0_gnn_Wrel3, L0_gnn_brel3, L0_gnn_Wroot3, L0_gnn_g0, L0_gnn_be0, L0_gnn_g1, L0_gnn_be1, L0_gnn_g2, L0_gnn_be2, L0_gnn_g3, L0_gnn_be3):
    import jax
    import jax.numpy as jnp

    def _L0_gnn_ref(x, edge_index, edge_weight, W1, b1, Wrel2, brel2, Wroot2, Wrel3, brel3, Wroot3, g0, be0, g1, be1, g2, be2, g3, be3):
        import jax, jax.numpy as jnp
        import numpy as np
        N_NODES = 50000
        N_EDGES = 12500
        C_IN, H1, H2 = (128, 256, 128)
        EPS = 1e-05

        def _bn(x, g, b):
            m = jnp.mean(x, axis=0)
            v = jnp.var(x, axis=0)
            return g * (x - m) * jax.lax.rsqrt(v + EPS) + b

        def _gcn_conv(x, src, dst, ew, W, b, n):
            xw = x @ W
            deg = jax.ops.segment_sum(ew, dst, num_segments=n) + 1.0
            dinv = jax.lax.rsqrt(deg)
            norm = dinv[src] * ew * dinv[dst]
            agg = jax.ops.segment_sum(norm[:, None] * xw[src], dst, num_segments=n)
            return agg + xw / deg[:, None] + b

        def _graph_conv(x, src, dst, ew, Wrel, brel, Wroot, n):
            agg = jax.ops.segment_sum(ew[:, None] * x[src], dst, num_segments=n)
            return agg @ Wrel + brel + x @ Wroot
        n = x.shape[0]
        src, dst = (edge_index[0], edge_index[1])
        xn = _bn(x, g0, be0)
        h = _bn(jax.nn.relu(_gcn_conv(xn, src, dst, edge_weight, W1, b1, n)), g1, be1)
        h = _bn(jax.nn.relu(_graph_conv(h, src, dst, edge_weight, Wrel2, brel2, Wroot2, n)), g2, be2)
        h = _bn(jax.nn.relu(_graph_conv(h, src, dst, edge_weight, Wrel3, brel3, Wroot3, n)), g3, be3)
        return h
    edge_index = jnp.stack([src, dst])
    h = jnp.maximum(_layernorm(x, axis=-1), 0.0)
    x = x + _L0_gnn_ref(h, edge_index, edge_weight, L0_gnn_W1, L0_gnn_b1, L0_gnn_Wrel2, L0_gnn_brel2, L0_gnn_Wroot2, L0_gnn_Wrel3, L0_gnn_brel3, L0_gnn_Wroot3, L0_gnn_g0, L0_gnn_be0, L0_gnn_g1, L0_gnn_be1, L0_gnn_g2, L0_gnn_be2, L0_gnn_g3, L0_gnn_be3)
    return x

_drawn_inputs = setup_inputs


def setup_inputs(seed=0):
    import zlib

    import numpy as np

    out = dict(_drawn_inputs(seed))
    spreads = {'L0_gnn_b1': (0.0, 0.1),
     'L0_gnn_brel2': (0.0, 0.1),
     'L0_gnn_brel3': (0.0, 0.1),
     'L0_gnn_g0': (1.0, 0.2),
     'L0_gnn_be0': (0.0, 0.1),
     'L0_gnn_g1': (1.0, 0.2),
     'L0_gnn_be1': (0.0, 0.1),
     'L0_gnn_g2': (1.0, 0.2),
     'L0_gnn_be2': (0.0, 0.1),
     'L0_gnn_g3': (1.0, 0.2),
     'L0_gnn_be3': (0.0, 0.1)}
    factors = {}
    for name, (base, spread) in spreads.items():
        noise = np.random.default_rng([zlib.crc32(name.encode()), seed]).standard_normal(out[name].shape)
        drawn = base * np.exp(spread * noise) if base else spread * noise
        out[name] = jnp.asarray(drawn.astype(out[name].dtype))
    for name, factor in factors.items():
        out[name] = (out[name] * factor).astype(out[name].dtype)
    return out
```

```python
from contextlib import ExitStack

import concourse.bass as bass
from concourse import mybir

FP = mybir.dt.float32
BF = mybir.dt.bfloat16
I32 = mybir.dt.int32
ALU = mybir.AluOpType
ACT = mybir.ActivationFunctionType

P = 125
C = 128
G = 8
W = P * G
EG = 4
CW = P * EG
CH = W // CW
NS = 4
ES = 2
EPS = 1e-5
MASK = -3.0e38


class Phase:

    def __init__(self, nc, name):
        self.nc, self.name, self.memory, self.sems = nc, name, ExitStack(), []

    def __enter__(self):
        return self

    def sb(self, name, shape, dt=FP):
        return self.memory.enter_context(self.nc.sbuf_tensor(f"{self.name}_{name}", shape, dt))

    def pb(self, name, banks):
        return self.memory.enter_context(self.nc.psum_tensor(f"{self.name}_{name}", [128, banks, 512], FP))

    def sem(self, name):
        s = self.memory.enter_context(self.nc.semaphore(f"{self.name}_{name}"))
        self.sems.append(s)
        return s

    def slots(self, name, n):
        return [self.sem(f"{name}{j}") for j in range(n)]

    def start(self):
        self.ctx = self.nc.Block()
        return self.ctx.__enter__()

    def __exit__(self, kind, *rest):
        if kind is None:
            self.ctx.__exit__(None, None, None)
            if self.sems:
                with self.nc.Block() as block:
                    @block.gpsimd
                    def _(pool):
                        for s in self.sems:
                            pool.sem_clear(s)
            self.memory.close()
        return False


def wait_use(eng, sem, i, per=1, upto=None, base=0):
    if isinstance(i, int) and i < 0:
        return
    eng.wait_ge(sem, i * per + (base + (per if upto is None else upto)))


def pipeline(eng, iters, slots, stages):
    def back(i, j, lag):
        return i - (lag - j + slots - 1) // slots if lag > j else i, (j - lag) % slots

    def round_(i):
        for j in range(slots):
            for lag, step in stages:
                at, slot = back(i, j, lag)
                if not (isinstance(at, int) and at < 0):
                    step(at, slot)

    round_(0)
    if iters > 1:
        with eng.Fori(1, iters) as i:
            round_(i)
    total = iters * slots
    for k in range(total, total + max(lag for lag, _ in stages)):
        for lag, step in stages:
            if k - lag < total:
                step((k - lag) // slots, (k - lag) % slots)


def before(i, j, d, slots):
    return i - (d - j + slots - 1) // slots if d > j else i, (j - d) % slots


def build(nc, x, src, dst, ew, prm, out):
    N, E = x.shape[0], src.shape[0]
    NT = N // W
    EC = E // CW
    ET = E // P
    DI, EI = NT // NS, EC // ES
    assert N == DI * NS * W and E == EI * ES * CW and DI > 1 and EI > 1
    H1 = prm["W1"].shape[1]
    BN = NT * CH + EC

    def dram(name, shape, dt=FP):
        return nc.dram_tensor(name, shape, dt, kind="Internal").ap()

    h0 = dram("h0_dense", (NT, C, 1, W))
    h1 = dram("h1_dense", (NT, C, 2, W))
    h2 = dram("h2_dense", (NT, C, 2, W))
    h3 = dram("h3_dense", (NT, C, 1, W))
    hs = [dram(f"h{n}_src", (EC, C, k, CW)) for n, k in ((0, 1), (1, 2), (2, 2))]
    hd = [dram(f"h{n}_dst", (EC, C, k, CW)) for n, k in ((0, 1), (1, 2), (2, 2), (3, 1))]
    agg = [None] + [dram(f"agg{n}", (EC, C, k, CW)) for n, k in ((1, 1), (2, 2), (3, 2))]
    tab = [None] + [dram(f"agg_rows{n}", (E + P, k * C)) for n, k in ((1, 1), (2, 2))]
    node_map = dram("node_map", (N + E, 2))
    r_same = dram("row_same", (E,))
    r_msg = dram("row_msg", (E,))
    r_isrc = dram("row_inv_deg_src", (E,))
    r_rdst = dram("row_rsqrt_deg_dst", (E,))
    r_idst = dram("row_inv_deg_dst", (E,))
    r_neg_edge = dram("row_neg_edge", (E,), BF)
    r_neg_node = dram("row_neg_node", (NT * G, P), BF)
    r_pos = dram("row_pos_src", (E,), I32)
    r_out = dram("row_out_node", (E,), I32)

    keep = ExitStack()
    with keep:
        def sb(name, shape, dt=FP):
            return keep.enter_context(nc.sbuf_tensor(name, shape, dt))

        ident = sb("ident", [128, 128])
        ones_row = sb("ones_row", [1, 128], BF)
        zero_row = sb("zero_row", [P, 2 * C])
        w1 = sb("w1", [C, 1, H1])
        wroot = [None, None, sb("wroot2", [C, 2, H1]), sb("wroot3", [C, 2, C])]
        wrel = [None, None, sb("wrel2", [C, 2, H1]), sb("wrel3", [C, 2, C])]
        wfold = [None, sb("w1_fold", [C, 1, H1]), sb("wroot2_fold", [C, 2, H1]), sb("wroot3_fold", [C, 2, C])]
        bias = [None] + [sb(f"bias{n}", [C, k]) for n, k in ((1, 2), (2, 2), (3, 1))]
        bfold = [None] + [sb(f"bias{n}_fold", [C, k]) for n, k in ((1, 2), (2, 2), (3, 1))]
        gam = [sb(f"gamma{n}", [C, k]) for n, k in enumerate((1, 2, 2, 1))]
        bet = [sb(f"beta{n}", [C, k]) for n, k in enumerate((1, 2, 2, 1))]
        sca = [sb(f"bn_scale{n}", [C, k]) for n, k in enumerate((1, 2, 2, 1))]
        sft = [sb(f"bn_shift{n}", [C, k]) for n, k in enumerate((1, 2, 2, 1))]
        stats = sb("bn_stats_all", [C, 2, BN, 6])
        src_c = sb("src_cols", [P, ET], I32)
        dst_c = sb("dst_cols", [P, ET], I32)
        pos_c = sb("pos_cols", [P, ET], I32)
        out_c = sb("out_cols", [P, ET], I32)
        mhalf = sb("minus_half", [128, max(ET, G)])
        row_in = [keep.enter_context(nc.semaphore(f"rows_gathered{j}")) for j in range(ES)]
        stood = {"in": 0, "out": 0}
        row_out = [keep.enter_context(nc.semaphore(f"rows_scattered{j}")) for j in range(ES)]

        with Phase(nc, "setup") as ph:
            wl, cst = ph.sem("weights_in"), ph.sem("constants")
            edge_in, fill = ph.sem("edges_in"), ph.sem("filled")
            ds, ps_, ob = ph.sem("dve_steps"), ph.sem("pe_steps"), ph.sem("rows_out")
            pw = ph.sem("pow_done")
            s_b = ph.sb("src_b", [P, ET], I32)
            d_b = ph.sb("dst_b", [P, ET], I32)
            dp_b = ph.sb("dst_prev", [P, ET], I32)
            dn_b = ph.sb("dst_next", [P, ET], I32)
            w_b = ph.sb("ew_b", [P, ET])
            pos_i = ph.sb("pos_i", [P, ET], I32)
            same = ph.sb("same", [P, ET])
            zeros = ph.sb("zeros", [P, ET])
            pa = ph.sb("prefix_all", [P, ET])
            sc = ph.sb("segsum", [P, ET])
            arow, brow = ph.sb("arow", [1, P]), ph.sb("brow", [1, P])
            crow = ph.sb("crow", [1, P + 1])
            carry = ph.sb("carry", [P, 1])
            last = ph.sb("last", [P, ET])
            mval = ph.sb("map_values", [P, ET, 2])
            pos_n = ph.sb("pos_n", [P, ET])
            dif = ph.sb("dif", [P, ET])
            sidx = ph.sb("scatter_idx", [P, ET], I32)
            neg = ph.sb("neg_edge", [P, ET], BF)
            rdst, idst = ph.sb("rdst", [P, ET]), ph.sb("idst", [P, ET])
            blank = ph.sb("map_blank", [P, N // P, 2])
            pst = ph.pb("ps", 1)
            pst2 = ph.pb("ps2", 1)
            pst3 = ph.pb("ps3", 1)
            block = ph.start()

            @block.sync
            def _(sp):
                sp.dma_start(s_b[:, :], src.rearrange("(p t) -> p t", t=ET)).then_inc(edge_in, 16)
                sp.dma_start(d_b[:, :], dst.rearrange("(p t) -> p t", t=ET)).then_inc(edge_in, 16)
                sp.dma_start(w_b[:, :], ew.rearrange("(p t) -> p t", t=ET)).then_inc(edge_in, 16)
                sp.wait_ge(fill, 2)
                sp.dma_start(dp_b[0:1, 1:ET], dst[0:ET - 1].rearrange("(a t) -> a t", a=1)).then_inc(edge_in, 16)
                sp.dma_start(dp_b[1:P, :], dst[ET - 1:E - 1].rearrange("(p t) -> p t", t=ET)).then_inc(edge_in, 16)
                sp.dma_start(dn_b[0:P - 1, :], dst[1:E - ET + 1].rearrange("(p t) -> p t", t=ET)).then_inc(edge_in, 16)
                sp.dma_start(dn_b[P - 1:P, 0:ET - 1], dst[E - ET + 1:E].rearrange("(a t) -> a t", a=1)).then_inc(edge_in, 16)
                sp.dma_start(src_c[:, :], src.rearrange("(t p) -> p t", p=P), allow_slow_non_contiguous=True).then_inc(wl, 16)
                sp.dma_start(dst_c[:, :], dst.rearrange("(t p) -> p t", p=P), allow_slow_non_contiguous=True).then_inc(wl, 16)
                sp.dma_start(w1[:, 0, :], prm["W1"]).then_inc(wl, 16)
                for t, name in ((wroot[2], "Wroot2"), (wroot[3], "Wroot3"), (wrel[2], "Wrel2"), (wrel[3], "Wrel3")):
                    sp.dma_start(t[:, :, :], prm[name].rearrange("(k p) n -> p k n", p=C)).then_inc(wl, 16)
                vectors = [(bias[1], "b1"), (bias[2], "brel2"), (bias[3], "brel3")]
                vectors += [(gam[n], f"g{n}") for n in range(4)] + [(bet[n], f"be{n}") for n in range(4)]
                for t, name in vectors:
                    sp.dma_start(t[:, :], prm[name].rearrange("(k p) -> p k", p=C), allow_slow_non_contiguous=True).then_inc(wl, 16)
                sp.wait_ge(wl, 16 * (7 + len(vectors)))
                sp.wait_ge(ds, 17)
                sp.wait_ge(pw, 1)
                flat = lambda r: r.rearrange("(p t) -> p t", t=ET)
                sp.dma_start(flat(r_same), same[:, :]).then_inc(ob, 16)
                sp.dma_start(flat(r_rdst), rdst[:, :]).then_inc(ob, 16)
                sp.dma_start(flat(r_idst), idst[:, :]).then_inc(ob, 16)
                sp.dma_start(flat(r_neg_edge), neg[:, :]).then_inc(ob, 16)
                sp.dma_start(flat(r_out), sidx[:, :]).then_inc(ob, 16)
                sp.wait_ge(cst, 8)
                sp.dma_start(node_map[0:N, :].rearrange("(p n) c -> p n c", p=P), blank[:, :, :]).then_inc(ob, 16)
                for n in (1, 2):
                    sp.dma_start(tab[n][E:E + P, :], zero_row[:, 0:n * C]).then_inc(ob, 16)
                sp.wait_ge(ob, 16 * 8)
                sp.dma_start(out_c[:, :], r_out.rearrange("(t p) -> p t", p=P), allow_slow_non_contiguous=True).then_inc(ob, 16)
                sp.wait_ge(ob, 16 * 9)

            @block.gpsimd
            def _(pool):
                pool.memset(dp_b[:, :], -1).then_inc(fill, 1)
                pool.memset(dn_b[:, :], -1).then_inc(fill, 1)
                pool.memset(ident[:, :], 0.0).then_inc(cst, 1)
                pool.memset(ones_row[:, :], 1.0).then_inc(cst, 1)
                pool.memset(zero_row[:, :], 0.0).then_inc(cst, 1)
                pool.memset(mhalf[:, :], -0.5).then_inc(cst, 1)
                pool.wait_ge(cst, 1)
                pool.affine_select(out=ident[:, :], in_=ident[:, :], compare_op=ALU.not_equal, fill=1.0,
                                   base=0, pattern=[[-1, 128]], channel_multiplier=1).then_inc(cst, 1)
                pool.iota(pos_i[:, :], pattern=[[1, ET]], base=0, channel_multiplier=ET).then_inc(cst, 1)
                pool.memset(blank[:, :, 0:1], float(E)).then_inc(cst, 1)
                pool.memset(blank[:, :, 1:2], 1.0).then_inc(cst, 1)
                pool.wait_ge(ds, 9)
                pool.wait_ge(cst, 8)
                pool.tensor_tensor(rdst[:, :], mval[:, :, 1], mhalf[0:P, 0:ET], ALU.pow).then_inc(pw, 1)

            @block.tensor
            def _(pe):
                pe.wait_ge(cst, 8)
                pe.wait_ge(ds, 4)
                pe.matmul(pst[0:1, 0, 0:P], pa[:, ET - 1:ET], ident[0:P, 0:P], start=True, stop=True).then_inc(ps_, 1)
                pe.matmul(pst2[0:1, 0, 0:P], sc[:, ET - 1:ET], ident[0:P, 0:P], start=True, stop=True).then_inc(ps_, 1)
                pe.wait_ge(ds, 7)
                pe.matmul(pst3[0:P, 0, 0:1], crow[0:1, 0:P], ident[0:1, 0:1], start=True, stop=True).then_inc(ps_, 1)

            @block.vector
            def _(dve):
                done = [0]

                def link(ins):
                    done[0] += 1
                    ins.then_inc(ds, 1)
                    dve.wait_ge(ds, done[0])

                link(dve.memset(zeros[:, :], 0.0))
                dve.wait_ge(edge_in, 16 * 7)
                link(dve.tensor_tensor(same[:, :], d_b[:, :], dp_b[:, :], ALU.is_equal))
                link(dve.tensor_tensor_scan(pa[:, :], same[:, :], zeros[:, :], 1.0, ALU.mult, ALU.add))
                link(dve.tensor_tensor_scan(sc[:, :], same[:, :], w_b[:, :], 0.0, ALU.mult, ALU.add))
                dve.memset(crow[:, :], 0.0).then_inc(ds, 1)
                done[0] += 1
                dve.wait_ge(ps_, 2)
                dve.tensor_copy(arow[:, :], pst[0:1, 0, 0:P])
                link(dve.tensor_copy(brow[:, :], pst2[0:1, 0, 0:P]))
                link(dve.tensor_tensor_scan(crow[:, 1:P + 1], arow[:, :], brow[:, :], 0.0, ALU.mult, ALU.add))
                dve.wait_ge(ps_, 3)
                link(dve.tensor_copy(carry[:, :], pst3[0:P, 0, 0:1]))
                dve.tensor_tensor_scan(dif[:, :], same[:, :], w_b[:, :], carry[:, 0:1], ALU.mult, ALU.add).then_inc(fill, 1)
                dve.wait_ge(fill, 3)
                link(dve.tensor_scalar(mval[:, :, 1], dif[:, :], 1.0, None, ALU.add))
                link(dve.reciprocal(idst[:, :], mval[:, :, 1]))
                link(dve.tensor_tensor(last[:, :], d_b[:, :], dn_b[:, :], ALU.not_equal))
                dve.wait_ge(cst, 8)
                link(dve.tensor_copy(mval[:, :, 0], pos_i[:, :]))
                link(dve.tensor_scalar(pos_n[:, :], pos_i[:, :], float(N), None, ALU.add))
                link(dve.tensor_tensor(dif[:, :], d_b[:, :], pos_n[:, :], ALU.subtract))
                link(dve.tensor_tensor(dif[:, :], dif[:, :], last[:, :], ALU.mult))
                link(dve.tensor_tensor(sidx[:, :], dif[:, :], pos_n[:, :], ALU.add))
                link(dve.tensor_scalar(neg[:, :], last[:, :], -MASK, MASK, ALU.mult, ALU.add))

            edge_tiles = (mval, sidx, s_b, w_b)

            ph.ctx.__exit__(None, None, None)
            MG = 5
            MI = ET // (2 * MG)
            assert ET == MI * 2 * MG and MI > 1
            cp, gate = ph.slots("copied", 2), ph.sem("gate")
            sdma, gdma, got = row_out, row_in, ph.slots("taken", 2)
            rows2, node_in, nd, npe = ph.sem("rows2"), ph.sem("node_in"), ph.sem("node_dve"), ph.sem("node_pe")
            node_out, pw2, msd = ph.slots("node_out", 2), ph.sem("pow2"), ph.sem("msteps")
            scat_done = ph.sem("scatter_done")
            cols = ph.sb("idx_slot", [P, 2, MG], I32)
            vals = ph.sb("val_slot", [P, 2, MG, 2])
            msrc = ph.sb("map_src", [P, ET, 2])
            rsrc, isrc, cmsg = ph.sb("rsrc", [P, ET]), ph.sb("isrc", [P, ET]), ph.sb("cmsg", [P, ET])
            posi = ph.sb("posi", [P, ET], I32)
            flags = ph.sb("flags", [P, NT * G])
            nmap = ph.sb("nmap", [P, NT, 2 * G])
            nrow = ph.sb("neg_rows", [128, 2, P], BF)
            blk = -(-(NT * G) // 128)
            ph.ctx = nc.Block()
            block = ph.ctx.__enter__()

            @block.gpsimd
            def _(pool):
                def scatter(i, j):
                    wait_use(pool, sdma[j], i - 1, 16 * MG)
                    pool.sem_inc(gate, 1)
                    pool.tensor_copy(cols[:, j, :], sidx[:, bass.ds((i * 2 + j) * MG, MG)]).then_inc(cp[j], 1)
                    pool.tensor_copy(vals[:, j, :, :], mval[:, bass.ds((i * 2 + j) * MG, MG), :]).then_inc(cp[j], 1)
                    wait_use(pool, cp[j], i, 2)
                    pool.sem_inc(gate, 1)
                    for m in range(MG):
                        pool.indirect_dma_start(node_map[:, :], bass.IndirectOffsetOnAxis(ap=cols[:, j, m:m + 1], axis=0),
                                                vals[:, j, m, :], None).then_inc(sdma[j], 16)

                pipeline(pool, MI, 2, [(0, scatter)])
                for j in range(2):
                    pool.wait_ge(sdma[j], 16 * MG * MI)
                pool.sem_inc(scat_done, 1)

                def gather(i, j):
                    wait_use(pool, got[j], i - 1)
                    pool.sem_inc(gate, 1)
                    pool.tensor_copy(cols[:, j, :], s_b[:, bass.ds((i * 2 + j) * MG, MG)]).then_inc(cp[j], 1)
                    pool.wait_ge(cp[j], 2 * MI + i + 1)
                    pool.sem_inc(gate, 1)
                    for m in range(MG):
                        pool.indirect_dma_start(vals[:, j, m, :], None, node_map[0:N, :],
                                                bass.IndirectOffsetOnAxis(ap=cols[:, j, m:m + 1], axis=0)).then_inc(gdma[j], 16)

                def take(i, j):
                    wait_use(pool, gdma[j], i, 16 * MG)
                    pool.sem_inc(gate, 1)
                    pool.tensor_copy(msrc[:, bass.ds((i * 2 + j) * MG, MG), :], vals[:, j, :, :]).then_inc(got[j], 1)

                pipeline(pool, MI, 2, [(0, gather), (1, take)])
                for j in range(2):
                    pool.wait_ge(got[j], MI)
                pool.tensor_tensor(rsrc[:, :], msrc[:, :, 1], mhalf[0:P, 0:ET], ALU.pow).then_inc(pw2, 1)

            @block.sync
            def _(sp):
                sp.wait_ge(scat_done, 1)
                sp.dma_start(nmap[:, :, :], node_map[0:N, :].rearrange("(t p g) c -> p t (g c)", p=P, g=G)).then_inc(node_in, 16)
                for b in range(blk):
                    n = min(128, NT * G - 128 * b)
                    sp.wait_ge(nd, b + 2)
                    sp.dma_start(r_neg_node[128 * b:128 * b + n, :], nrow[0:n, b % 2, :]).then_inc(node_out[b % 2], 16)
                sp.wait_ge(msd, 3)
                flat = lambda r: r.rearrange("(p t) -> p t", t=ET)
                sp.dma_start(flat(r_msg), cmsg[:, :]).then_inc(rows2, 16)
                sp.dma_start(flat(r_isrc), isrc[:, :]).then_inc(rows2, 16)
                sp.dma_start(flat(r_pos), posi[:, :]).then_inc(rows2, 16)
                sp.wait_ge(rows2, 48)
                sp.dma_start(pos_c[:, :], r_pos.rearrange("(t p) -> p t", p=P), allow_slow_non_contiguous=True).then_inc(rows2, 16)
                sp.wait_ge(rows2, 64)
                for j in range(min(2, blk)):
                    sp.wait_ge(node_out[j], 16 * ((blk - j + 1) // 2))

            @block.tensor
            def _(pe):
                pe.wait_ge(nd, 1)
                for b in range(blk):
                    n = min(128, NT * G - 128 * b)
                    if b >= 2:
                        pe.wait_ge(nd, b)
                    pe.matmul((pst, pst2)[b % 2][0:n, 0, 0:P], flags[:, 128 * b:128 * b + n], ident[0:P, 0:P],
                              start=True, stop=True).then_inc(npe, 1)

            @block.vector
            def _(dve):
                dve.wait_ge(node_in, 16)
                dve.tensor_scalar(flags[:, :].rearrange("p (t g) -> p t g", g=G),
                                  nmap[:, :, :].rearrange("p t (g c) -> p t g c", c=2)[:, :, :, 0],
                                  float(E), None, ALU.is_lt).then_inc(nd, 1)
                for b in range(blk):
                    n = min(128, NT * G - 128 * b)
                    dve.wait_ge(npe, b + 1)
                    if b >= 2:
                        dve.wait_ge(node_out[b % 2], 16 * (b // 2))
                    dve.tensor_scalar(nrow[0:n, b % 2, :], (pst, pst2)[b % 2][0:n, 0, 0:P], MASK, None, ALU.mult).then_inc(nd, 1)
                for j in range(2):
                    dve.wait_ge(got[j], MI)
                dve.reciprocal(isrc[:, :], msrc[:, :, 1]).then_inc(msd, 1)
                dve.tensor_copy(posi[:, :], msrc[:, :, 0]).then_inc(msd, 1)
                dve.wait_ge(pw2, 1)
                dve.tensor_tensor(cmsg[:, :], w_b[:, :], rsrc[:, :], ALU.mult).then_inc(msd, 1)

        stood["in"] = stood["out"] = 16 * MG * MI

        def layer_norm(name, iters, slots, groups, x_rows, idx, dest, with_stats):
            banks = groups * P // CW
            base = 0 if idx is None else stood["in"]
            stood["in"] += 0 if idx is None else 16 * groups * iters
            with Phase(nc, name) as ph:
                got, copied, gate = ph.slots("rows", slots) if idx is None else row_in, ph.slots("copied", slots), ph.sem("gate")
                var, nrm, hn = ph.slots("var", slots), ph.slots("norm", slots), ph.slots("hn", slots)
                tr, rl, st, sto = ph.slots("transposed", slots), ph.slots("relu", slots), ph.slots("stat", slots), ph.slots("stored", slots)
                step = ph.slots("ln_step", slots)
                xt = ph.sb("x", [P, slots, groups, C])
                cols = ph.sb("idx", [P, slots, groups], I32)
                bs = ph.sb("bs", [P, slots, groups, 6])
                sm, df, q = (ph.sb(n, [P, slots, groups]) for n in ("sum", "dif", "q"))
                ve, nm = ph.sb("ve", [P, slots, groups]), ph.sb("nmean", [P, slots, groups])
                rs, nb = ph.sb("rstd", [P, slots, groups]), ph.sb("nbias", [P, slots, groups])
                xn = ph.sb("xn", [P, slots, groups, C])
                ho = ph.sb("ho", [C, slots, groups * P])
                ps = ph.pb("ps", 2 * banks)
                block = ph.start()
                back = min(slots - 1, 3)

                @block.sync
                def _(sp):
                    def load(i, j):
                        wait_use(sp, hn[j], i - 1)
                        k = i * slots + j
                        sp.dma_start(xt[0:120, j, :, :], x_rows[k, 0:120]).then_inc(got[j], 16)
                        sp.dma_start(xt[120:P, j, :, :], x_rows[k, 120:P]).then_inc(got[j], 16)

                    def store(i, j):
                        wait_use(sp, rl[j], i, banks)
                        sp.dma_start(dest[i * slots + j].rearrange("c a w -> c (a w)"), ho[:, j, :]).then_inc(sto[j], 16)

                    pipeline(sp, iters, slots, ([(0, load)] if idx is None else []) + [(back, store)])
                    for j in range(slots):
                        sp.wait_ge(sto[j], 16 * iters)

                parts = 32 if idx is None else 16 * groups

                @block.gpsimd
                def _(pool):
                    def gather(i, j):
                        wait_use(pool, hn[j], i - 1)
                        pool.sem_inc(gate, 1)
                        pool.tensor_copy(cols[:, j, :], idx[:, bass.ds((i * slots + j) * groups, groups)]).then_inc(copied[j], 1)
                        wait_use(pool, copied[j], i)
                        pool.sem_inc(gate, 1)
                        for g in range(groups):
                            pool.indirect_dma_start(xt[:, j, g, :], None, x[:, :],
                                                    bass.IndirectOffsetOnAxis(ap=cols[:, j, g:g + 1], axis=0)).then_inc(got[j], 16)

                    def scale(i, j):
                        wait_use(pool, var[j], i)
                        pool.tensor_tensor(rs[:, j, :], ve[:, j, :], mhalf[0:P, 0:groups], ALU.pow).then_inc(nrm[j], 1)
                        wait_use(pool, nrm[j], i, 2, 1)
                        pool.tensor_tensor(nb[:, j, :], nm[:, j, :], rs[:, j, :], ALU.mult).then_inc(nrm[j], 1)

                    pipeline(pool, iters, slots, ([] if idx is None else [(0, gather)]) + [(0 if idx is None else 1, scale)])

                @block.vector
                def _(dve):
                    def moments(i, j):
                        wait_use(dve, got[j], i, parts, base=base)
                        for g in range(groups):
                            ins = dve.bn_stats(bs[:, j, g, :], xt[:, j, g, :])
                        ins.then_inc(step[j], 1)
                        wait_use(dve, step[j], i, 3, 1)
                        dve.tensor_tensor(sm[:, j, :], bs[:, j, :, 1], bs[:, j, :, 4], ALU.add)
                        dve.tensor_tensor(df[:, j, :], bs[:, j, :, 1], bs[:, j, :, 4], ALU.subtract)
                        dve.tensor_tensor(q[:, j, :], bs[:, j, :, 2], bs[:, j, :, 5], ALU.add).then_inc(step[j], 1)
                        wait_use(dve, step[j], i, 3, 2)
                        dve.tensor_scalar(nm[:, j, :], sm[:, j, :], -0.5, None, ALU.mult)
                        dve.tensor_scalar(q[:, j, :], q[:, j, :], 1.0 / C, EPS, ALU.mult, ALU.add)
                        dve.scalar_tensor_tensor(df[:, j, :], df[:, j, :], 0.25, df[:, j, :], ALU.mult, ALU.mult).then_inc(step[j], 1)
                        wait_use(dve, step[j], i, 3, 3)
                        dve.tensor_tensor(ve[:, j, :], q[:, j, :], df[:, j, :], ALU.add).then_inc(var[j], 1)

                    def gather_stats(i, j):
                        for b in range(banks):
                            wait_use(dve, rl[j], i, banks, b + 1)
                            dve.sem_inc(gate, 1)
                            dve.bn_stats(stats[:, 0, (i * slots + j) * banks + b, :], ho[:, j, b * CW:(b + 1) * CW]).then_inc(st[j], 1)

                    pipeline(dve, iters, slots, [(0, moments)] + ([(2, gather_stats)] if with_stats else []))

                @block.scalar
                def _(act):
                    def normalise(i, j):
                        wait_use(act, nrm[j], i, 2)
                        wait_use(act, tr[j], i - 1, banks)
                        for g in range(groups):
                            ins = act.activation(xn[:, j, g, :], xt[:, j, g, :], ACT.Identity,
                                                 bias=nb[:, j, g:g + 1], scale=rs[:, j, g:g + 1])
                        ins.then_inc(hn[j], 1)

                    def relu(i, j):
                        wait_use(act, sto[j], i - 1, 16)
                        if with_stats:
                            wait_use(act, st[j], i - 1, banks)
                        for b in range(banks):
                            wait_use(act, tr[j], i, banks, b + 1)
                            act.activation(ho[:, j, b * CW:(b + 1) * CW], ps[:, (j % 2) * banks + b, 0:CW], ACT.Relu).then_inc(rl[j], 1)

                    pipeline(act, iters, slots, [(0, normalise), (1, relu)])

                @block.tensor
                def _(pe):
                    def turn(i, j):
                        wait_use(pe, hn[j], i)
                        i2, j2 = before(i, j, 2, slots)
                        wait_use(pe, rl[j2], i2, banks)
                        for b in range(banks):
                            for g in range(EG):
                                ins = pe.transpose(ps[:, (j % 2) * banks + b, g * P:(g + 1) * P], xn[:, j, b * EG + g, :], ident[0:P, 0:P])
                            ins.then_inc(tr[j], 1)

                    pipeline(pe, iters, slots, [(0, turn)])

        x_tiles = x.rearrange("(t p g) c -> t p g c", p=P, g=G)
        layer_norm("ln_dense", DI, NS, G, x_tiles, None, h0, True)
        layer_norm("ln_src", EI, ES, EG, None, src_c, hs[0], False)
        layer_norm("ln_dst", EI, ES, EG, None, dst_c, hd[0], False)

        def fold(n, blocks, groups, weight, folded, b_in, b_out):
            ratio = groups * CW / N
            with Phase(nc, f"fold{n}") as ph:
                s, pwd, pd = ph.sem("steps"), ph.sem("pow"), ph.sem("bias")
                mv = ph.sb("mv", [C, blocks, 2])
                t1, t2, t3 = (ph.sb(f"t{k}", [C, blocks]) for k in (1, 2, 3))
                ps = ph.pb("ps", 2)
                block = ph.start()
                marks = {}

                @block.vector
                def _(dve):
                    done = [0]

                    def link(ins):
                        done[0] += 1
                        ins.then_inc(s, 1)
                        dve.wait_ge(s, done[0])

                    for b in range(blocks):
                        link(dve.bn_aggr(mv[:, b, :], stats[:, b, 0:groups, :].rearrange("p g s -> p (g s)")))
                    mean, var = mv[:, :, 0], mv[:, :, 1]
                    link(dve.tensor_tensor(t1[:, :], mean, mean, ALU.mult))
                    link(dve.tensor_tensor(t2[:, :], var, t1[:, :], ALU.add))
                    link(dve.tensor_scalar(t2[:, :], t2[:, :], ratio, None, ALU.mult))
                    link(dve.tensor_scalar(t1[:, :], mean, ratio, None, ALU.mult))
                    link(dve.tensor_tensor(t3[:, :], t1[:, :], t1[:, :], ALU.mult))
                    link(dve.tensor_tensor(t2[:, :], t2[:, :], t3[:, :], ALU.subtract))
                    link(dve.tensor_scalar(t2[:, :], t2[:, :], 0.0, EPS, ALU.max, ALU.add))
                    marks["var"] = done[0]
                    dve.wait_ge(pwd, 1)
                    link(dve.tensor_tensor(sca[n][:, :], gam[n][:, :], t3[:, :], ALU.mult))
                    link(dve.tensor_tensor(t1[:, :], t1[:, :], sca[n][:, :], ALU.mult))
                    link(dve.tensor_tensor(sft[n][:, :], bet[n][:, :], t1[:, :], ALU.subtract))
                    marks["shift"] = done[0]
                    if weight is None:
                        return
                    for k in range(blocks):
                        link(dve.tensor_scalar(folded[:, k, :], weight[:, k, :], sca[n][:, k:k + 1], None, ALU.mult))
                    for m in range(b_in.shape[1]):
                        dve.wait_ge(pd, m + 1)
                        link(dve.tensor_tensor(b_out[:, m:m + 1], b_in[:, m:m + 1], ps[:, m, 0:1], ALU.add))

                @block.gpsimd
                def _(pool):
                    pool.wait_ge(s, blocks + 7)
                    pool.tensor_tensor(t3[:, :], t2[:, :], mhalf[:, 0:blocks], ALU.pow).then_inc(pwd, 1)

                @block.tensor
                def _(pe):
                    if weight is None:
                        return
                    pe.wait_ge(s, blocks + 10)
                    for m in range(b_in.shape[1]):
                        for k in range(blocks):
                            ins = pe.matmul(ps[:, m, 0:1], weight[:, k, m * C:(m + 1) * C], sft[n][:, k:k + 1],
                                            start=k == 0, stop=k == blocks - 1)
                        ins.then_inc(pd, 1)

        def aggregate(n, kb):
            rows = n < 3
            banks = kb
            with Phase(nc, f"agg{n}") as ph:
                got, aff, msg = ph.slots("in", ES), ph.slots("affine", ES), ph.slots("msg", ES)
                scn, agd = ph.slots("scan", ES), ph.slots("agg", ES)
                tr, ev, sto, stt = ph.slots("transposed", ES), ph.slots("evac", ES), ph.slots("stored", ES), ph.slots("rows_out", ES)
                hi = ph.sb("h", [C, ES, kb, CW])
                xa = ph.sb("xa", [C, ES, kb, CW])
                sm, cf, rd = (ph.sb(f"row{k}", [C, ES, CW]) for k in range(3))
                se = ph.sb("scan", [C, ES, kb, CW])
                ag = ph.sb("agg", [C, ES, kb, CW]) if n == 1 else se
                tb = ph.sb("tb", [P, ES, EG, kb * C])
                first = ph.sb("first", [C, 1])
                f0 = ph.sem("first")
                ps = ph.pb("ps", ES * banks)
                per_bank = EG // banks
                block = ph.start()
                r_coef = r_msg if n == 1 else ew
                loads = 48 + 16 * (n == 1)
                tiles = tab[n][0:E, :].rearrange("(t g p) c -> t p g c", p=P, g=EG) if rows else None
                full = agd if n == 1 else scn

                @block.sync
                def _(sp):
                    def load(i, j):
                        k = i * ES + j
                        wait_use(sp, msg[j], i - 1, kb)
                        wait_use(sp, full[j], i - 1, kb)
                        sp.dma_start(hi[:, j, :, :], hs[n - 1][k]).then_inc(got[j], 16)
                        for t, r in ((sm, r_same), (cf, r_coef)) + (((rd, r_rdst),) if n == 1 else ()):
                            line = r.rearrange("(k o w) -> k o w", o=1, w=CW)[k]
                            sp.dma_start(t[:, j, :], line.broadcast_to([C, CW])).then_inc(got[j], 16)

                    def store(i, j):
                        k = i * ES + j
                        wait_use(sp, full[j], i, kb)
                        sp.dma_start(agg[n][k], ag[:, j, :, :]).then_inc(sto[j], 16)

                    def store_rows(i, j):
                        wait_use(sp, ev[j], i, banks)
                        sp.dma_start(tiles[i * ES + j], tb[:, j, :, :]).then_inc(stt[j], 16)

                    pipeline(sp, EI, ES, [(0, load), (1, store)] + ([(1, store_rows)] if rows else []))
                    for j in range(ES):
                        sp.wait_ge(sto[j], 16 * EI)
                        if rows:
                            sp.wait_ge(stt[j], 16 * EI)

                @block.scalar
                def _(act):
                    def affine(i, j):
                        wait_use(act, got[j], i, loads)
                        wait_use(act, msg[j], i - 1, kb)
                        for k in range(kb):
                            act.activation(xa[:, j, k, :], hi[:, j, k, :], ACT.Identity, bias=sft[n - 1][:, k:k + 1],
                                           scale=sca[n - 1][:, k:k + 1]).then_inc(aff[j], 1)

                    def evacuate(i, j):
                        wait_use(act, stt[j], i - 1, 16)
                        for b in range(banks):
                            wait_use(act, tr[j], i, banks, b + 1)
                            act.activation(tb[:, j, b * per_bank:(b + 1) * per_bank, :],
                                           ps[0:P, j * banks + b, 0:per_bank * kb * C].rearrange("p (g c) -> p g c", g=per_bank),
                                           ACT.Copy).then_inc(ev[j], 1)

                    pipeline(act, EI, ES, [(0, affine)] + ([(1, evacuate)] if rows else []))

                @block.vector
                def _(dve):
                    dve.memset(first[:, :], 0.0).then_inc(f0, 1)
                    dve.wait_ge(f0, 1)

                    def sums(i, j):
                        wait_use(dve, got[j], i, loads)
                        for k in range(kb):
                            wait_use(dve, aff[j], i, kb, k + 1)
                            dve.tensor_tensor(xa[:, j, k, :], xa[:, j, k, :], cf[:, j, :], ALU.mult).then_inc(msg[j], 1)
                        wait_use(dve, sto[j], i - 1, 16)
                        if rows:
                            wait_use(dve, tr[j], i - 1, banks)
                        ip, jp = before(i, j, 1, ES)
                        wait_use(dve, scn[jp], ip, kb)
                        for k in range(kb):
                            wait_use(dve, msg[j], i, kb, k + 1)
                            fresh = isinstance(ip, int) and ip < 0
                            start = first[:, 0:1] if fresh else se[:, jp, k, CW - 1:CW]
                            dve.tensor_tensor_scan(se[:, j, k, :], sm[:, j, :], xa[:, j, k, :], start, ALU.mult, ALU.add).then_inc(scn[j], 1)
                        if n == 1:
                            for k in range(kb):
                                wait_use(dve, scn[j], i, kb, k + 1)
                                dve.tensor_tensor(ag[:, j, k, :], se[:, j, k, :], rd[:, j, :], ALU.mult).then_inc(agd[j], 1)

                    pipeline(dve, EI, ES, [(0, sums)])

                @block.tensor
                def _(pe):
                    if not rows:
                        return

                    def turn(i, j):
                        wait_use(pe, full[j], i, kb)
                        wait_use(pe, ev[j], i - 1, banks)
                        for b in range(banks):
                            for g in range(per_bank):
                                for k in range(kb):
                                    e = (b * per_bank + g) * P
                                    ins = pe.transpose(ps[0:P, j * banks + b, (g * kb + k) * C:(g * kb + k + 1) * C],
                                                       ag[:, j, k, e:e + P], ident[:, :])
                            ins.then_inc(tr[j], 1)

                    pipeline(pe, EI, ES, [(0, turn)])

        def dense_layer(n, kb, mb, h_in, h_out):
            wf, bf = wfold[n], bfold[n]
            per = mb * CH
            with Phase(nc, f"dense{n}") as ph:
                got, mm, rl = ph.slots("in", NS), ph.slots("product", NS), ph.slots("relu", NS)
                st, sto, gate = ph.slots("stat", NS), ph.slots("stored", NS), ph.sem("gate")
                hi = ph.sb("hi", [C, NS, kb, W])
                ho = ph.sb("ho", [C, NS, mb, W])
                mk = ph.sb("mask", [1, NS, W], BF)
                ps = ph.pb("ps", 2 * per)
                masks = r_neg_node.rearrange("(t g) p -> t (g p)", g=G).rearrange("(t o) w -> t o w", o=1)
                block = ph.start()

                @block.sync
                def _(sp):
                    def load(i, j):
                        wait_use(sp, mm[j], i - 1, per)
                        k = i * NS + j
                        sp.dma_start(hi[:, j, :, :], h_in[k]).then_inc(got[j], 16)
                        sp.dma_start(mk[:, j, :], masks[k]).then_inc(got[j], 16)

                    def store(i, j):
                        wait_use(sp, rl[j], i, per)
                        sp.dma_start(h_out[i * NS + j], ho[:, j, :, :]).then_inc(sto[j], 16)

                    pipeline(sp, DI, NS, [(0, load), (3, store)])
                    for j in range(NS):
                        sp.wait_ge(sto[j], 16 * DI)

                @block.tensor
                def _(pe):
                    def products(i, j):
                        wait_use(pe, got[j], i, 32)
                        i2, j2 = before(i, j, 2, NS)
                        for m in range(mb):
                            for c in range(CH):
                                bank = (j % 2) * per + m * CH + c
                                wait_use(pe, rl[j2], i2, per, m * CH + c + 1)
                                pe.matmul(ps[:, bank, 0:CW], ones_row[:, :], mk[:, j, c * CW:(c + 1) * CW], start=True, stop=False)
                                for k in range(kb):
                                    ins = pe.matmul(ps[:, bank, 0:CW], wf[:, k, m * C:(m + 1) * C],
                                                    hi[:, j, k, c * CW:(c + 1) * CW], start=False, stop=k == kb - 1)
                                ins.then_inc(mm[j], 1)

                    pipeline(pe, DI, NS, [(0, products)])

                @block.scalar
                def _(act):
                    def relu(i, j):
                        wait_use(act, sto[j], i - 1, 16)
                        wait_use(act, st[j], i - 1, per)
                        for m in range(mb):
                            for c in range(CH):
                                wait_use(act, mm[j], i, per, m * CH + c + 1)
                                act.activation(ho[:, j, m, c * CW:(c + 1) * CW], ps[:, (j % 2) * per + m * CH + c, 0:CW],
                                               ACT.Relu, bias=bf[:, m:m + 1]).then_inc(rl[j], 1)

                    pipeline(act, DI, NS, [(0, relu)])

                @block.vector
                def _(dve):
                    def statistics(i, j):
                        for m in range(mb):
                            for c in range(CH):
                                wait_use(dve, rl[j], i, per, m * CH + c + 1)
                                dve.sem_inc(gate, 1)
                                dve.bn_stats(stats[:, m, (i * NS + j) * CH + c, :], ho[:, j, m, c * CW:(c + 1) * CW]).then_inc(st[j], 1)

                    pipeline(dve, DI, NS, [(0, statistics)])

        def edge_layer(n, kb, mb, of_dst, h_in, h_out):
            first = n == 1
            w_root, b_use = (w1, bias[1]) if first else (wfold[n], bfold[n])
            loads = 16 * (1 + first + 2 * of_dst)
            base = stood["in"]
            stood["in"] += 0 if of_dst else 16 * EG * EI
            with Phase(nc, f"{'dst' if of_dst else 'src'}{n}") as ph:
                got, cpd, gth, gate = ph.slots("in", ES), ph.slots("copied", ES), row_in, ph.sem("gate")
                gat2 = ph.sem("gate2")
                tr, ad, aff, dv = ph.slots("transposed", ES), ph.slots("agg", ES), ph.slots("affine", ES), ph.slots("scaled", ES)
                mm, rl, st, sto = ph.slots("product", ES), ph.slots("relu", ES), ph.slots("stat", ES), ph.slots("stored", ES)
                hi = ph.sb("hi", [C, ES, kb, CW])
                ag = ph.sb("ag", [C, ES, kb, CW])
                z = ph.sb("z", [C, ES, kb, CW]) if first else None
                inv = ph.sb("inv", [C, ES, CW]) if first else None
                mk = ph.sb("mask", [1, ES, CW], BF)
                tg = ph.sb("rows", [P, ES, EG, kb * C])
                cols = ph.sb("idx", [P, ES, EG], I32)
                ho = ph.sb("ho", [C, ES, mb, CW])
                pt = ph.pb("pt", ES * kb)
                ps = ph.pb("ps", ES * mb)
                block = ph.start()
                ready = dv if first else ad
                ready_n = 2 * kb if first else kb

                @block.sync
                def _(sp):
                    def load(i, j):
                        k = i * ES + j
                        wait_use(sp, mm[j], i - 1, mb)
                        sp.dma_start(hi[:, j, :, :], h_in[k]).then_inc(got[j], 16)
                        if of_dst:
                            sp.dma_start(ag[:, j, :, :], agg[n][k]).then_inc(got[j], 16)
                            sp.dma_start(mk[:, j, :], r_neg_edge.rearrange("(k o w) -> k o w", o=1, w=CW)[k]).then_inc(got[j], 16)
                        if first:
                            line = (r_idst if of_dst else r_isrc).rearrange("(k o w) -> k o w", o=1, w=CW)[k]
                            sp.dma_start(inv[:, j, :], line.broadcast_to([C, CW])).then_inc(got[j], 16)

                    def store(i, j):
                        wait_use(sp, rl[j], i, mb)
                        sp.dma_start(h_out[i * ES + j], ho[:, j, :, :]).then_inc(sto[j], 16)

                    pipeline(sp, EI, ES, [(0, load), (1, store)])
                    for j in range(ES):
                        sp.wait_ge(sto[j], 16 * EI)

                @block.gpsimd
                def _(pool):
                    if of_dst:
                        return

                    def gather(i, j):
                        wait_use(pool, tr[j], i - 1, kb)
                        pool.sem_inc(gate, 1)
                        pool.tensor_copy(cols[:, j, :], pos_c[:, bass.ds((i * ES + j) * EG, EG)]).then_inc(cpd[j], 1)
                        wait_use(pool, cpd[j], i)
                        pool.sem_inc(gate, 1)
                        for g in range(EG):
                            pool.indirect_dma_start(tg[:, j, g, :], None, tab[n][:, :],
                                                    bass.IndirectOffsetOnAxis(ap=cols[:, j, g:g + 1], axis=0)).then_inc(gth[j], 16)

                    pipeline(pool, EI, ES, [(0, gather)])

                @block.tensor
                def _(pe):
                    def turn(i, j):
                        wait_use(pe, gth[j], i, 16 * EG, base=base)
                        for k in range(kb):
                            wait_use(pe, ready[j] if first else ad[j], i - 1, ready_n)
                            for g in range(EG):
                                ins = pe.transpose(pt[:, j * kb + k, g * P:(g + 1) * P], tg[:, j, g, k * C:(k + 1) * C], ident[0:P, 0:P])
                            ins.then_inc(tr[j], 1)

                    def products(i, j):
                        wait_use(pe, got[j], i, loads)
                        if first or not of_dst:
                            wait_use(pe, ready[j], i, ready_n)
                        wait_use(pe, rl[j], i - 1, mb)
                        for m in range(mb):
                            o = ps[:, j * mb + m, 0:CW]
                            mc = slice(m * C, (m + 1) * C)
                            if of_dst:
                                pe.matmul(o, ones_row[:, :], mk[:, j, :], start=True, stop=False)
                            terms = [(w_root[:, k, mc], (z if first else hi)[:, j, k, :]) for k in range(kb)]
                            if not first:
                                terms += [(wrel[n][:, k, mc], ag[:, j, k, :]) for k in range(kb)]
                            for t, (a, b) in enumerate(terms):
                                ins = pe.matmul(o, a, b, start=t == 0 and not of_dst, stop=t == len(terms) - 1)
                            ins.then_inc(mm[j], 1)

                    pipeline(pe, EI, ES, ([] if of_dst else [(0, turn)]) + [(0 if of_dst else 1, products)])

                @block.vector
                def _(dve):
                    def aggregate_in(i, j):
                        if first:
                            wait_use(dve, got[j], i, loads)
                            wait_use(dve, mm[j], i - 1, mb)
                            for k in range(kb):
                                wait_use(dve, aff[j], i, kb, k + 1)
                                dve.tensor_tensor(z[:, j, k, :], z[:, j, k, :], inv[:, j, :], ALU.mult).then_inc(dv[j], 1)
                            for k in range(kb):
                                wait_use(dve, dv[j], i, 2 * kb, k + 1)
                                if not of_dst:
                                    wait_use(dve, tr[j], i, kb, k + 1)
                                a = ag[:, j, k, :] if of_dst else pt[:, j * kb + k, 0:CW]
                                dve.tensor_tensor(z[:, j, k, :], z[:, j, k, :], a, ALU.add).then_inc(dv[j], 1)
                        elif not of_dst:
                            wait_use(dve, mm[j], i - 1, mb)
                            for k in range(kb):
                                wait_use(dve, tr[j], i, kb, k + 1)
                                dve.tensor_copy(ag[:, j, k, :], pt[:, j * kb + k, 0:CW]).then_inc(ad[j], 1)

                    def statistics(i, j):
                        for m in range(mb):
                            wait_use(dve, rl[j], i, mb, m + 1)
                            dve.sem_inc(gat2, 1)
                            dve.bn_stats(stats[:, m, NT * CH + i * ES + j, :], ho[:, j, m, :]).then_inc(st[j], 1)

                    stages = ([(0, aggregate_in)] if first or not of_dst else []) + ([(1, statistics)] if of_dst else [])
                    pipeline(dve, EI, ES, stages)

                @block.scalar
                def _(act):
                    def affine(i, j):
                        wait_use(act, got[j], i, loads)
                        wait_use(act, mm[j], i - 1, mb)
                        for k in range(kb):
                            act.activation(z[:, j, k, :], hi[:, j, k, :], ACT.Identity, bias=sft[0][:, k:k + 1],
                                           scale=sca[0][:, k:k + 1]).then_inc(aff[j], 1)

                    def relu(i, j):
                        wait_use(act, sto[j], i - 1, 16)
                        if of_dst:
                            wait_use(act, st[j], i - 1, mb)
                        for m in range(mb):
                            wait_use(act, mm[j], i, mb, m + 1)
                            act.activation(ho[:, j, m, :], ps[:, j * mb + m, 0:CW], ACT.Relu, bias=b_use[:, m:m + 1]).then_inc(rl[j], 1)

                    pipeline(act, EI, ES, ([(0, affine)] if first else []) + [(1, relu)])

        def output(name, iters, slots, groups, h_in, x_rows, out_rows):
            banks = groups // EG
            dense = x_rows is not None
            gbase, sbase = (0, 0) if dense else (stood["in"], stood["out"])
            with Phase(nc, name) as ph:
                got, gx, cpd, gate = ph.slots("in", slots), ph.slots("x", slots) if dense else row_in, ph.slots("copied", slots), ph.sem("gate")
                aff, tr, sm, sto = ph.slots("affine", slots), ph.slots("transposed", slots), ph.slots("summed", slots), ph.slots("stored", slots) if dense else row_out
                hi = ph.sb("hi", [C, slots, groups * P])
                xt = ph.sb("x", [P, slots, groups, C])
                ot = ph.sb("out", [P, slots, groups, C])
                cols = ph.sb("idx", [P, slots, 2 * groups], I32)
                ps = ph.pb("ps", 2 * banks)
                back = min(slots - 1, 3)
                block = ph.start()

                @block.sync
                def _(sp):
                    def load(i, j):
                        k = i * slots + j
                        wait_use(sp, tr[j], i - 1, banks)
                        sp.dma_start(hi[:, j, :], h_in[k].rearrange("c a w -> c (a w)")).then_inc(got[j], 16)
                        if dense:
                            wait_use(sp, sm[j], i - 1, banks)
                            sp.dma_start(xt[0:120, j, :, :], x_rows[k, 0:120]).then_inc(gx[j], 16)
                            sp.dma_start(xt[120:P, j, :, :], x_rows[k, 120:P]).then_inc(gx[j], 16)

                    def store(i, j):
                        k = i * slots + j
                        wait_use(sp, sm[j], i, banks)
                        sp.dma_start(out_rows[k, 0:120], ot[0:120, j, :, :]).then_inc(sto[j], 16)
                        sp.dma_start(out_rows[k, 120:P], ot[120:P, j, :, :]).then_inc(sto[j], 16)

                    pipeline(sp, iters, slots, [(0, load)] + ([(back, store)] if dense else []))
                    if dense:
                        for j in range(slots):
                            sp.wait_ge(sto[j], 32 * iters)

                @block.gpsimd
                def _(pool):
                    if dense:
                        return

                    def gather(i, j):
                        wait_use(pool, sto[j], i - 1, 16 * groups, base=sbase)
                        pool.sem_inc(gate, 1)
                        at = bass.ds((i * slots + j) * groups, groups)
                        pool.tensor_copy(cols[:, j, 0:groups], dst_c[:, at]).then_inc(cpd[j], 1)
                        pool.tensor_copy(cols[:, j, groups:2 * groups], out_c[:, at]).then_inc(cpd[j], 1)
                        wait_use(pool, cpd[j], i, 2)
                        pool.sem_inc(gate, 1)
                        for g in range(groups):
                            pool.indirect_dma_start(xt[:, j, g, :], None, x[:, :],
                                                    bass.IndirectOffsetOnAxis(ap=cols[:, j, g:g + 1], axis=0)).then_inc(gx[j], 16)

                    def scatter(i, j):
                        wait_use(pool, sm[j], i, banks)
                        pool.sem_inc(gate, 1)
                        for g in range(groups):
                            pool.indirect_dma_start(out[:, :], bass.IndirectOffsetOnAxis(ap=cols[:, j, groups + g:groups + g + 1], axis=0),
                                                    ot[:, j, g, :], None).then_inc(sto[j], 16)

                    pipeline(pool, iters, slots, [(0, gather), (1, scatter)])
                    for j in range(slots):
                        pool.wait_ge(sto[j], sbase + 16 * groups * iters)

                @block.scalar
                def _(act):
                    def affine(i, j):
                        wait_use(act, got[j], i, 16)
                        act.activation(hi[:, j, :], hi[:, j, :], ACT.Identity, bias=sft[3][:, 0:1], scale=sca[3][:, 0:1]).then_inc(aff[j], 1)

                    pipeline(act, iters, slots, [(0, affine)])

                @block.tensor
                def _(pe):
                    def turn(i, j):
                        wait_use(pe, aff[j], i)
                        i2, j2 = before(i, j, 2, slots)
                        wait_use(pe, sm[j2], i2, banks)
                        for b in range(banks):
                            for g in range(EG):
                                e = (b * EG + g) * P
                                ins = pe.transpose(ps[0:P, (j % 2) * banks + b, g * C:(g + 1) * C], hi[:, j, e:e + P], ident[:, :])
                            ins.then_inc(tr[j], 1)

                    pipeline(pe, iters, slots, [(0, turn)])

                @block.vector
                def _(dve):
                    def add(i, j):
                        wait_use(dve, gx[j], i, 32 if dense else 16 * groups, base=gbase)
                        wait_use(dve, sto[j], i - 1, 32 if dense else 16 * groups, base=sbase)
                        for b in range(banks):
                            wait_use(dve, tr[j], i, banks, b + 1)
                            dve.tensor_tensor(ot[:, j, b * EG:(b + 1) * EG, :],
                                              ps[0:P, (j % 2) * banks + b, 0:EG * C].rearrange("p (g c) -> p g c", g=EG),
                                              xt[:, j, b * EG:(b + 1) * EG, :], ALU.add).then_inc(sm[j], 1)

                    pipeline(dve, iters, slots, [(0, add)])

        fold(0, 1, NT * CH, w1, wfold[1], bias[1], bfold[1])
        aggregate(1, 1)
        edge_layer(1, 1, 2, True, hd[0], hd[1])
        edge_layer(1, 1, 2, False, hs[0], hs[1])
        dense_layer(1, 1, 2, h0, h1)
        fold(1, 2, BN, wroot[2], wfold[2], bias[2], bfold[2])
        aggregate(2, 2)
        edge_layer(2, 2, 2, True, hd[1], hd[2])
        edge_layer(2, 2, 2, False, hs[1], hs[2])
        dense_layer(2, 2, 2, h1, h2)
        fold(2, 2, BN, wroot[3], wfold[3], bias[3], bfold[3])
        aggregate(3, 2)
        edge_layer(3, 2, 1, True, hd[2], hd[3])
        dense_layer(3, 2, 1, h2, h3)
        fold(3, 1, BN, None, None, None, None)
        output("out_dense", DI, NS, G, h3, x_tiles, out[0:N, :].rearrange("(t p g) c -> t p g c", p=P, g=G))
        output("out_dst", EI, ES, EG, hd[3], None, None)


def kernel(**inputs):
    import numpy as np
    import concourse.bacc as bacc
    from concourse.bass_utils import run_bass_kernel_spmd as run

    nc = bacc.Bacc("TRN2", target_bir_lowering=False, num_devices=1)
    arrays, aps = {}, {}
    for name in inputs:
        a = np.ascontiguousarray(inputs[name])
        arrays["in_" + name] = a
        aps[name] = nc.dram_tensor("in_" + name, a.shape, mybir.dt.from_np(a.dtype), kind="ExternalInput").ap()
    n, e = inputs["x"].shape[0], inputs["src"].shape[0]
    out = nc.dram_tensor("out", (n + e, C), FP, kind="ExternalOutput").ap()
    prm = {name[len("L0_gnn_"):]: aps[name] for name in inputs if name.startswith("L0_gnn_")}
    build(nc, aps["x"], aps["src"], aps["dst"], aps["edge_weight"], prm, out)
    r = run(nc, [arrays], core_ids=[0])
    return r.results[0]["out"][:n]
```

```python
from contextlib import ExitStack

import concourse.bass as bass
from concourse import mybir

FP = mybir.dt.float32
BF = mybir.dt.bfloat16
I32 = mybir.dt.int32
ALU = mybir.AluOpType
ACT = mybir.ActivationFunctionType

P = 125
C = 128
G = 8
W = P * G
EG = 4
CW = P * EG
CH = W // CW
NS = 4
ES = 2
QS = 4
QG = EG // 2
EPS = 1e-5
MASK = -3.0e38


class Phase:

    def __init__(self, nc, name):
        self.nc, self.name, self.memory, self.sems = nc, name, ExitStack(), []

    def __enter__(self):
        return self

    def sb(self, name, shape, dt=FP):
        return self.memory.enter_context(self.nc.sbuf_tensor(f"{self.name}_{name}", shape, dt))

    def pb(self, name, banks):
        return self.memory.enter_context(self.nc.psum_tensor(f"{self.name}_{name}", [128, banks, 512], FP))

    def sem(self, name):
        s = self.memory.enter_context(self.nc.semaphore(f"{self.name}_{name}"))
        self.sems.append(s)
        return s

    def slots(self, name, n):
        return [self.sem(f"{name}{j}") for j in range(n)]

    def start(self):
        self.ctx = self.nc.Block()
        return self.ctx.__enter__()

    def __exit__(self, kind, *rest):
        if kind is None:
            self.ctx.__exit__(None, None, None)
            if self.sems:
                with self.nc.Block() as block:
                    @block.gpsimd
                    def _(pool):
                        for s in self.sems:
                            pool.sem_clear(s)
            self.memory.close()
        return False


def wait_use(eng, sem, i, per=1, upto=None, base=0):
    if isinstance(i, int) and i < 0:
        return
    eng.wait_ge(sem, i * per + (base + (per if upto is None else upto)))


def pipeline(eng, rounds, streams):
    streams = [x for x in streams if x[1]]
    if not streams:
        return
    most = max(slots for slots, _ in streams)
    extra = max(-(-lag // slots) for slots, stages in streams for lag, _ in stages)

    def round_(i):
        for turn in range(most):
            for slots, stages in streams:
                if (turn + 1) * slots % most:
                    continue
                j = (turn + 1) * slots // most - 1
                for lag, step in stages:
                    at, slot = before(i, j, lag, slots)
                    if not isinstance(at, int) or 0 <= at < rounds:
                        step(at, slot)

    peeled = min(extra + 1, rounds)
    for i in range(peeled):
        round_(i)
    if peeled < rounds:
        with eng.Fori(peeled, rounds) as i:
            round_(i)
    for i in range(rounds, rounds + extra):
        round_(i)


def side_by_side(ph, rounds, works):
    block = ph.start()

    def run(eng, name):
        parts = [w[name](eng) for w in works if name in w]
        if parts:
            pipeline(eng, rounds, [(slots, stages) for slots, stages, _ in parts])
            for _, _, end in parts:
                if end:
                    end()

    @block.sync
    def _(sp):
        run(sp, "sync")

    @block.gpsimd
    def _(pool):
        run(pool, "gpsimd")

    @block.scalar
    def _(act):
        run(act, "scalar")

    @block.tensor
    def _(pe):
        run(pe, "tensor")

    @block.vector
    def _(dve):
        run(dve, "vector")


def before(i, j, d, slots):
    return i - (d - j + slots - 1) // slots if d > j else i, (j - d) % slots


def build(nc, x, src, dst, ew, prm, out):
    N, E = x.shape[0], src.shape[0]
    NT = N // W
    EC = E // CW
    ET = E // P
    DI, EI = NT // NS, EC // ES
    assert N == DI * NS * W and E == EI * ES * CW and DI > 1 and EI > 1
    H1 = prm["W1"].shape[1]
    BN = NT * CH + EC

    def dram(name, shape, dt=FP):
        return nc.dram_tensor(name, shape, dt, kind="Internal").ap()

    h0 = dram("h0_dense", (NT, C, 1, W))
    h1 = dram("h1_dense", (NT, C, 2, W))
    h2 = dram("h2_dense", (NT, C, 2, W))
    h3 = dram("h3_dense", (NT, C, 1, W))
    hs = [dram(f"h{n}_src", (EC, C, k, CW)) for n, k in ((0, 1), (1, 2), (2, 2))]
    hd = [dram(f"h{n}_dst", (EC, C, k, CW)) for n, k in ((0, 1), (1, 2), (2, 2), (3, 1))]
    tab = [None] + [dram(f"agg_rows{n}", (E + P, k * C)) for n, k in ((1, 1), (2, 2))]
    node_map = dram("node_map", (N + E, 2))
    r_same = dram("row_same", (E,), BF)
    r_msg = dram("row_msg", (E,))
    r_isrc = dram("row_inv_deg_src", (E,))
    r_rdst = dram("row_rsqrt_deg_dst", (E,))
    r_neg_edge = dram("row_neg_edge", (E,), BF)
    r_neg_node = dram("row_neg_node", (NT * G, P), BF)
    r_pos = dram("row_pos_src", (E,), I32)
    r_out = dram("row_out_node", (E,), I32)

    keep = ExitStack()
    with keep:
        def sb(name, shape, dt=FP):
            return keep.enter_context(nc.sbuf_tensor(name, shape, dt))

        ident = sb("ident", [128, 128])
        ones_row = sb("ones_row", [1, 128], BF)
        zero_row = sb("zero_row", [P, 2 * C])
        w1 = sb("w1", [C, 1, H1])
        wroot = [None, None, sb("wroot2", [C, 2, H1]), sb("wroot3", [C, 2, C])]
        wrel = [None, None, sb("wrel2", [C, 2, H1]), sb("wrel3", [C, 2, C])]
        wfold = [None, sb("w1_fold", [C, 1, H1]), sb("wroot2_fold", [C, 2, H1]), sb("wroot3_fold", [C, 2, C])]
        bias = [None] + [sb(f"bias{n}", [C, k]) for n, k in ((1, 2), (2, 2), (3, 1))]
        bfold = [None] + [sb(f"bias{n}_fold", [C, k]) for n, k in ((1, 2), (2, 2), (3, 1))]
        gam = [sb(f"gamma{n}", [C, k]) for n, k in enumerate((1, 2, 2, 1))]
        bet = [sb(f"beta{n}", [C, k]) for n, k in enumerate((1, 2, 2, 1))]
        mval = sb("map_values", [P, ET, 2])
        sidx = sb("scatter_idx", [P, ET], I32)
        s_b = sb("src_b", [P, ET], I32)
        w_b = sb("ew_b", [P, ET])
        sca = [sb(f"bn_scale{n}", [C, k]) for n, k in enumerate((1, 2, 2, 1))]
        sft = [sb(f"bn_shift{n}", [C, k]) for n, k in enumerate((1, 2, 2, 1))]
        stats = sb("bn_stats_all", [C, 2, BN, 6])
        src_c = sb("src_cols", [P, ET], I32)
        dst_c = sb("dst_cols", [P, ET], I32)
        pos_c = sb("pos_cols", [P, ET], I32)
        out_c = sb("out_cols", [P, ET], I32)
        mhalf = sb("minus_half", [128, max(ET, G)])
        msrc = sb("map_src", [P, ET, 2])
        gathered = {key: [keep.enter_context(nc.semaphore(f"sw_{key}{j}")) for j in range(QS)]
                    for key in ("ln", "map_out", "map_in", "src", "x", "out")}
        stood = {"ln": 0, "src": 0}

        with Phase(nc, "setup") as ph:
            wl, cst = ph.sem("weights_in"), ph.sem("constants")
            edge_in, fill = ph.sem("edges_in"), ph.sem("filled")
            ds, ps_, ob = ph.sem("dve_steps"), ph.sem("pe_steps"), ph.sem("rows_out")
            pw = ph.sem("pow_done")
            d_b = ph.sb("dst_b", [P, ET], I32)
            dp_b = ph.sb("dst_prev", [P, ET], I32)
            dn_b = ph.sb("dst_next", [P, ET], I32)
            pos_i = ph.sb("pos_i", [P, ET], I32)
            same = ph.sb("same", [P, ET])
            zeros = ph.sb("zeros", [P, ET])
            pa = ph.sb("prefix_all", [P, ET])
            sc = ph.sb("segsum", [P, ET])
            arow, brow = ph.sb("arow", [1, P]), ph.sb("brow", [1, P])
            crow = ph.sb("crow", [1, P + 1])
            carry = ph.sb("carry", [P, 1])
            last = ph.sb("last", [P, ET])
            pos_n = ph.sb("pos_n", [P, ET])
            dif = ph.sb("dif", [P, ET])
            neg = ph.sb("neg_edge", [P, ET], BF)
            rdst = ph.sb("rdst", [P, ET])
            same_row = ph.sb("same_row", [P, ET], BF)
            blank = ph.sb("map_blank", [P, N // P, 2])
            pst = ph.pb("ps", 1)
            pst2 = ph.pb("ps2", 1)
            pst3 = ph.pb("ps3", 1)
            block = ph.start()

            @block.sync
            def _(sp):
                sp.dma_start(s_b[:, :], src.rearrange("(p t) -> p t", t=ET)).then_inc(edge_in, 16)
                sp.dma_start(d_b[:, :], dst.rearrange("(p t) -> p t", t=ET)).then_inc(edge_in, 16)
                sp.dma_start(w_b[:, :], ew.rearrange("(p t) -> p t", t=ET)).then_inc(edge_in, 16)
                sp.wait_ge(fill, 2)
                sp.dma_start(dp_b[0:1, 1:ET], dst[0:ET - 1].rearrange("(a t) -> a t", a=1)).then_inc(edge_in, 16)
                sp.dma_start(dp_b[1:P, :], dst[ET - 1:E - 1].rearrange("(p t) -> p t", t=ET)).then_inc(edge_in, 16)
                sp.dma_start(dn_b[0:P - 1, :], dst[1:E - ET + 1].rearrange("(p t) -> p t", t=ET)).then_inc(edge_in, 16)
                sp.dma_start(dn_b[P - 1:P, 0:ET - 1], dst[E - ET + 1:E].rearrange("(a t) -> a t", a=1)).then_inc(edge_in, 16)
                sp.dma_start(src_c[:, :], src.rearrange("(t p) -> p t", p=P), allow_slow_non_contiguous=True).then_inc(wl, 16)
                sp.dma_start(dst_c[:, :], dst.rearrange("(t p) -> p t", p=P), allow_slow_non_contiguous=True).then_inc(wl, 16)
                sp.dma_start(w1[:, 0, :], prm["W1"]).then_inc(wl, 16)
                for t, name in ((wroot[2], "Wroot2"), (wroot[3], "Wroot3"), (wrel[2], "Wrel2"), (wrel[3], "Wrel3")):
                    sp.dma_start(t[:, :, :], prm[name].rearrange("(k p) n -> p k n", p=C)).then_inc(wl, 16)
                vectors = [(bias[1], "b1"), (bias[2], "brel2"), (bias[3], "brel3")]
                vectors += [(gam[n], f"g{n}") for n in range(4)] + [(bet[n], f"be{n}") for n in range(4)]
                for t, name in vectors:
                    sp.dma_start(t[:, :], prm[name].rearrange("(k p) -> p k", p=C), allow_slow_non_contiguous=True).then_inc(wl, 16)
                sp.wait_ge(wl, 16 * (7 + len(vectors)))
                sp.wait_ge(ds, 17)
                sp.wait_ge(pw, 1)
                flat = lambda r: r.rearrange("(p t) -> p t", t=ET)
                sp.dma_start(flat(r_same), same_row[:, :]).then_inc(ob, 16)
                sp.dma_start(flat(r_rdst), rdst[:, :]).then_inc(ob, 16)
                sp.dma_start(flat(r_neg_edge), neg[:, :]).then_inc(ob, 16)
                sp.dma_start(flat(r_out), sidx[:, :]).then_inc(ob, 16)
                sp.wait_ge(cst, 8)
                sp.dma_start(node_map[0:N, :].rearrange("(p n) c -> p n c", p=P), blank[:, :, :]).then_inc(ob, 16)
                for n in (1, 2):
                    sp.dma_start(tab[n][E:E + P, :], zero_row[:, 0:n * C]).then_inc(ob, 16)
                sp.wait_ge(ob, 16 * 7)
                sp.dma_start(out_c[:, :], r_out.rearrange("(t p) -> p t", p=P), allow_slow_non_contiguous=True).then_inc(ob, 16)
                sp.wait_ge(ob, 16 * 8)

            @block.gpsimd
            def _(pool):
                pool.memset(dp_b[:, :], -1).then_inc(fill, 1)
                pool.memset(dn_b[:, :], -1).then_inc(fill, 1)
                pool.memset(ident[:, :], 0.0).then_inc(cst, 1)
                pool.memset(ones_row[:, :], 1.0).then_inc(cst, 1)
                pool.memset(zero_row[:, :], 0.0).then_inc(cst, 1)
                pool.memset(mhalf[:, :], -0.5).then_inc(cst, 1)
                pool.wait_ge(cst, 1)
                pool.affine_select(out=ident[:, :], in_=ident[:, :], compare_op=ALU.not_equal, fill=1.0,
                                   base=0, pattern=[[-1, 128]], channel_multiplier=1).then_inc(cst, 1)
                pool.iota(pos_i[:, :], pattern=[[1, ET]], base=0, channel_multiplier=ET).then_inc(cst, 1)
                pool.memset(blank[:, :, 0:1], float(E)).then_inc(cst, 1)
                pool.memset(blank[:, :, 1:2], 1.0).then_inc(cst, 1)
                pool.wait_ge(ds, 9)
                pool.wait_ge(cst, 8)
                pool.tensor_tensor(rdst[:, :], mval[:, :, 1], mhalf[0:P, 0:ET], ALU.pow).then_inc(pw, 1)

            @block.tensor
            def _(pe):
                pe.wait_ge(cst, 8)
                pe.wait_ge(ds, 4)
                pe.matmul(pst[0:1, 0, 0:P], pa[:, ET - 1:ET], ident[0:P, 0:P], start=True, stop=True).then_inc(ps_, 1)
                pe.matmul(pst2[0:1, 0, 0:P], sc[:, ET - 1:ET], ident[0:P, 0:P], start=True, stop=True).then_inc(ps_, 1)
                pe.wait_ge(ds, 7)
                pe.matmul(pst3[0:P, 0, 0:1], crow[0:1, 0:P], ident[0:1, 0:1], start=True, stop=True).then_inc(ps_, 1)

            @block.vector
            def _(dve):
                done = [0]

                def link(ins):
                    done[0] += 1
                    ins.then_inc(ds, 1)
                    dve.wait_ge(ds, done[0])

                link(dve.memset(zeros[:, :], 0.0))
                dve.wait_ge(edge_in, 16 * 7)
                link(dve.tensor_tensor(same[:, :], d_b[:, :], dp_b[:, :], ALU.is_equal))
                link(dve.tensor_tensor_scan(pa[:, :], same[:, :], zeros[:, :], 1.0, ALU.mult, ALU.add))
                link(dve.tensor_tensor_scan(sc[:, :], same[:, :], w_b[:, :], 0.0, ALU.mult, ALU.add))
                dve.memset(crow[:, :], 0.0).then_inc(ds, 1)
                done[0] += 1
                dve.wait_ge(ps_, 2)
                dve.tensor_copy(arow[:, :], pst[0:1, 0, 0:P])
                link(dve.tensor_copy(brow[:, :], pst2[0:1, 0, 0:P]))
                link(dve.tensor_tensor_scan(crow[:, 1:P + 1], arow[:, :], brow[:, :], 0.0, ALU.mult, ALU.add))
                dve.wait_ge(ps_, 3)
                link(dve.tensor_copy(carry[:, :], pst3[0:P, 0, 0:1]))
                dve.tensor_tensor_scan(dif[:, :], same[:, :], w_b[:, :], carry[:, 0:1], ALU.mult, ALU.add).then_inc(fill, 1)
                dve.wait_ge(fill, 3)
                link(dve.tensor_scalar(mval[:, :, 1], dif[:, :], 1.0, None, ALU.add))
                link(dve.tensor_copy(same_row[:, :], same[:, :]))
                link(dve.tensor_tensor(last[:, :], d_b[:, :], dn_b[:, :], ALU.not_equal))
                dve.wait_ge(cst, 8)
                link(dve.tensor_copy(mval[:, :, 0], pos_i[:, :]))
                link(dve.tensor_scalar(pos_n[:, :], pos_i[:, :], float(N), None, ALU.add))
                link(dve.tensor_tensor(dif[:, :], d_b[:, :], pos_n[:, :], ALU.subtract))
                link(dve.tensor_tensor(dif[:, :], dif[:, :], last[:, :], ALU.mult))
                link(dve.tensor_tensor(sidx[:, :], dif[:, :], pos_n[:, :], ALU.add))
                link(dve.tensor_scalar(neg[:, :], last[:, :], -MASK, MASK, ALU.mult, ALU.add))

        assert DI == EI
        x_tiles = x.rearrange("(t p g) c -> t p g c", p=P, g=G)
        masks_dense = r_neg_node.rearrange("(t g) p -> t (g p)", g=G).rearrange("(t o) w -> t o w", o=1)
        by_chunk = lambda row: row.rearrange("(k o w) -> k o w", o=1, w=CW)

        def layer_norm(ph, name, slots, groups, idx, dest, banks_at, with_stats):
            dense = idx is None
            banks = max(groups * P // CW, 1)
            gb = groups // banks
            bw = gb * P
            base = 0 if dense else stood["ln"]
            got = ph.slots(f"{name}_rows", slots) if dense else gathered["ln"]
            copied, gate = ph.slots(f"{name}_copied", slots), ph.sem(f"{name}_gate")
            var, nrm, hn = (ph.slots(f"{name}_{n}", slots) for n in ("var", "norm", "hn"))
            tr, rl, sto, step = (ph.slots(f"{name}_{n}", slots) for n in ("transposed", "relu", "stored", "step"))
            st = ph.slots(f"{name}_stat", slots)
            xt = ph.sb(f"{name}_x", [P, slots, groups, C])
            cols = ph.sb(f"{name}_idx", [P, slots, groups], I32)
            bs = ph.sb(f"{name}_bs", [P, slots, groups, 6])
            sm, df, q, ve, nm, rs, nb = (ph.sb(f"{name}_{n}", [P, slots, groups])
                                         for n in ("sum", "dif", "q", "ve", "nmean", "rstd", "nbias"))
            xn = ph.sb(f"{name}_xn", [P, slots, groups, C])
            ho = ph.sb(f"{name}_ho", [C, slots, groups * P])
            ps, bank0, ring = banks_at
            l_mom, l_nrm, l_relu = (0, 1, 2) if dense else (2, 3, 4)
            parts = 32 if dense else 16 * groups
            rounds = DI if dense else EI
            if not dense:
                stood["ln"] += 16 * groups * EI

            def bank(j, b):
                return bank0 + (j % ring) * banks + b

            def sync(sp):
                def load(i, j):
                    wait_use(sp, hn[j], i - 1)
                    k = i * slots + j
                    sp.dma_start(xt[0:120, j, :, :], x_tiles[k, 0:120]).then_inc(got[j], 16)
                    sp.dma_start(xt[120:P, j, :, :], x_tiles[k, 120:P]).then_inc(got[j], 16)

                def store(i, j):
                    if dense:
                        to = dest[i * slots + j]
                    else:
                        to = dest[i * ES + j // 2][:, :, j % 2 * bw:(j % 2 + 1) * bw]
                    wait_use(sp, rl[j], i, banks)
                    sp.dma_start(to.rearrange("c a w -> c (a w)"), ho[:, j, :]).then_inc(sto[j], 16)

                def end():
                    for j in range(slots):
                        sp.wait_ge(sto[j], 16 * rounds)

                return slots, ([(0, load)] if dense else []) + [(l_relu + 3, store)], end

            def gpsimd(pool):
                def gather(i, j):
                    wait_use(pool, hn[j], i - 1)
                    pool.sem_inc(gate, 1)
                    pool.tensor_copy(cols[:, j, :], idx[:, bass.ds((i * slots + j) * groups, groups)]).then_inc(copied[j], 1)
                    wait_use(pool, copied[j], i)
                    pool.sem_inc(gate, 1)
                    for g in range(groups):
                        pool.indirect_dma_start(xt[:, j, g, :], None, x[:, :],
                                                bass.IndirectOffsetOnAxis(ap=cols[:, j, g:g + 1], axis=0)).then_inc(got[j], 16)

                def scale(i, j):
                    wait_use(pool, var[j], i)
                    pool.tensor_tensor(rs[:, j, :], ve[:, j, :], mhalf[0:P, 0:groups], ALU.pow).then_inc(nrm[j], 1)
                    wait_use(pool, nrm[j], i, 2, 1)
                    pool.tensor_tensor(nb[:, j, :], nm[:, j, :], rs[:, j, :], ALU.mult).then_inc(nrm[j], 1)

                return slots, [(0, scale)] if dense else [(0, gather), (l_mom, scale)], None

            def vector(dve):
                def moments(i, j):
                    wait_use(dve, got[j], i, parts, base=base)
                    for g in range(groups):
                        ins = dve.bn_stats(bs[:, j, g, :], xt[:, j, g, :])
                    ins.then_inc(step[j], 1)
                    wait_use(dve, step[j], i, 3, 1)
                    dve.tensor_tensor(sm[:, j, :], bs[:, j, :, 1], bs[:, j, :, 4], ALU.add)
                    dve.tensor_tensor(df[:, j, :], bs[:, j, :, 1], bs[:, j, :, 4], ALU.subtract)
                    dve.tensor_tensor(q[:, j, :], bs[:, j, :, 2], bs[:, j, :, 5], ALU.add).then_inc(step[j], 1)
                    wait_use(dve, step[j], i, 3, 2)
                    dve.tensor_scalar(nm[:, j, :], sm[:, j, :], -0.5, None, ALU.mult)
                    dve.tensor_scalar(q[:, j, :], q[:, j, :], 1.0 / C, EPS, ALU.mult, ALU.add)
                    dve.scalar_tensor_tensor(df[:, j, :], df[:, j, :], 0.25, df[:, j, :], ALU.mult, ALU.mult).then_inc(step[j], 1)
                    wait_use(dve, step[j], i, 3, 3)
                    dve.tensor_tensor(ve[:, j, :], q[:, j, :], df[:, j, :], ALU.add).then_inc(var[j], 1)

                def column_stats(i, j):
                    for b in range(banks):
                        wait_use(dve, rl[j], i, banks, b + 1)
                        dve.sem_inc(gate, 1)
                        dve.bn_stats(stats[:, 0, (i * slots + j) * banks + b, :], ho[:, j, b * CW:(b + 1) * CW]).then_inc(st[j], 1)

                return slots, [(l_mom, moments)] + ([(3, column_stats)] if with_stats else []), None

            def scalar(act):
                def normalise(i, j):
                    wait_use(act, nrm[j], i, 2)
                    wait_use(act, tr[j], i - 1, banks)
                    for g in range(groups):
                        ins = act.activation(xn[:, j, g, :], xt[:, j, g, :], ACT.Identity,
                                             bias=nb[:, j, g:g + 1], scale=rs[:, j, g:g + 1])
                    ins.then_inc(hn[j], 1)

                def relu(i, j):
                    wait_use(act, sto[j], i - 1, 16)
                    if with_stats:
                        wait_use(act, st[j], i - 1, banks)
                    for b in range(banks):
                        wait_use(act, tr[j], i, banks, b + 1)
                        act.activation(ho[:, j, b * bw:(b + 1) * bw], ps[:, bank(j, b), 0:bw], ACT.Relu).then_inc(rl[j], 1)

                return slots, [(l_nrm, normalise), (l_relu, relu)], None

            def tensor(pe):
                def turn(i, j):
                    wait_use(pe, hn[j], i)
                    i2, j2 = before(i, j, ring, slots)
                    wait_use(pe, rl[j2], i2, banks)
                    for b in range(banks):
                        for g in range(gb):
                            ins = pe.transpose(ps[:, bank(j, b), g * P:(g + 1) * P], xn[:, j, b * gb + g, :], ident[0:P, 0:P])
                        ins.then_inc(tr[j], 1)

                return slots, [(l_nrm, turn)], None

            return dict(sync=sync, gpsimd=gpsimd, vector=vector, scalar=scalar, tensor=tensor)

        def map_scatter(ph):
            cp, gate, sem = ph.slots("ms_copied", QS), ph.sem("ms_gate"), gathered["map_out"]
            cols, vals = ph.sb("ms_idx", [P, QS, QG], I32), ph.sb("ms_val", [P, QS, QG, 2])

            def gpsimd(pool):
                def scatter(i, j):
                    wait_use(pool, sem[j], i - 1, 16 * QG)
                    pool.sem_inc(gate, 1)
                    at = bass.ds((i * QS + j) * QG, QG)
                    pool.tensor_copy(cols[:, j, :], sidx[:, at]).then_inc(cp[j], 1)
                    pool.tensor_copy(vals[:, j, :, :], mval[:, at, :]).then_inc(cp[j], 1)
                    wait_use(pool, cp[j], i, 2)
                    pool.sem_inc(gate, 1)
                    for m in range(QG):
                        pool.indirect_dma_start(node_map[:, :], bass.IndirectOffsetOnAxis(ap=cols[:, j, m:m + 1], axis=0),
                                                vals[:, j, m, :], None).then_inc(sem[j], 16)

                def end():
                    for j in range(QS):
                        pool.wait_ge(sem[j], 16 * QG * EI)

                return QS, [(0, scatter)], end

            return dict(gpsimd=gpsimd)

        def map_gather(ph):
            cp, gate, got = ph.slots("mg_copied", QS), ph.sem("mg_gate"), ph.slots("mg_taken", QS)
            sem = gathered["map_in"]
            cols, vals = ph.sb("mg_idx", [P, QS, QG], I32), ph.sb("mg_val", [P, QS, QG, 2])

            def gpsimd(pool):
                def gather(i, j):
                    wait_use(pool, got[j], i - 1)
                    pool.sem_inc(gate, 1)
                    pool.tensor_copy(cols[:, j, :], s_b[:, bass.ds((i * QS + j) * QG, QG)]).then_inc(cp[j], 1)
                    wait_use(pool, cp[j], i)
                    pool.sem_inc(gate, 1)
                    for m in range(QG):
                        pool.indirect_dma_start(vals[:, j, m, :], None, node_map[0:N, :],
                                                bass.IndirectOffsetOnAxis(ap=cols[:, j, m:m + 1], axis=0)).then_inc(sem[j], 16)

                def take(i, j):
                    wait_use(pool, sem[j], i, 16 * QG)
                    pool.sem_inc(gate, 1)
                    pool.tensor_copy(msrc[:, bass.ds((i * QS + j) * QG, QG), :], vals[:, j, :, :]).then_inc(got[j], 1)

                return QS, [(0, gather), (2, take)], None

            return dict(gpsimd=gpsimd)

        def dense_layer(ph, n, kb, mb, h_in, h_out, ps):
            wf, bf = wfold[n], bfold[n]
            per = mb * CH
            got, mm, rl = ph.slots("dn_in", NS), ph.slots("dn_product", NS), ph.slots("dn_relu", NS)
            st, sto, gate = ph.slots("dn_stat", NS), ph.slots("dn_stored", NS), ph.sem("dn_gate")
            hi = ph.sb("dn_hi", [C, NS, kb, W])
            ho = ph.sb("dn_ho", [C, NS, mb, W])
            mk = ph.sb("dn_mask", [1, NS, W], BF)

            def sync(sp):
                def load(i, j):
                    wait_use(sp, mm[j], i - 1, per)
                    k = i * NS + j
                    sp.dma_start(hi[:, j, :, :], h_in[k]).then_inc(got[j], 16)
                    sp.dma_start(mk[:, j, :], masks_dense[k]).then_inc(got[j], 16)

                def store(i, j):
                    wait_use(sp, rl[j], i, per)
                    sp.dma_start(h_out[i * NS + j], ho[:, j, :, :]).then_inc(sto[j], 16)

                def end():
                    for j in range(NS):
                        sp.wait_ge(sto[j], 16 * DI)

                return NS, [(0, load), (3, store)], end

            def tensor(pe):
                def products(i, j):
                    wait_use(pe, got[j], i, 32)
                    for u in range(per):
                        m, c = divmod(u, CH)
                        if u >= 2:
                            wait_use(pe, rl[j], i, per, u - 1)
                        else:
                            i1, j1 = before(i, j, 1, NS)
                            wait_use(pe, rl[j1], i1, per, per - 1 + u)
                        o = ps[:, u % 2, 0:CW]
                        pe.matmul(o, ones_row[:, :], mk[:, j, c * CW:(c + 1) * CW], start=True, stop=False)
                        for k in range(kb):
                            ins = pe.matmul(o, wf[:, k, m * C:(m + 1) * C], hi[:, j, k, c * CW:(c + 1) * CW],
                                            start=False, stop=k == kb - 1)
                        ins.then_inc(mm[j], 1)

                return NS, [(0, products)], None

            def scalar(act):
                def relu(i, j):
                    wait_use(act, sto[j], i - 1, 16)
                    wait_use(act, st[j], i - 1, per)
                    for u in range(per):
                        m, c = divmod(u, CH)
                        wait_use(act, mm[j], i, per, u + 1)
                        act.activation(ho[:, j, m, c * CW:(c + 1) * CW], ps[:, u % 2, 0:CW],
                                       ACT.Relu, bias=bf[:, m:m + 1]).then_inc(rl[j], 1)

                return NS, [(0, relu)], None

            def vector(dve):
                def statistics(i, j):
                    for u in range(per):
                        m, c = divmod(u, CH)
                        wait_use(dve, rl[j], i, per, u + 1)
                        dve.sem_inc(gate, 1)
                        dve.bn_stats(stats[:, m, (i * NS + j) * CH + c, :], ho[:, j, m, c * CW:(c + 1) * CW]).then_inc(st[j], 1)

                return NS, [(0, statistics)], None

            return dict(sync=sync, tensor=tensor, scalar=scalar, vector=vector)

        def edge_layer(ph, n, ps):
            kb, mb = (1, 2, 2)[n - 1], (2, 2, 1)[n - 1]
            ks = n - 1
            l_turn, l_src, l_sum, l_rel, l_dst, l_out = {1: (0, 0, 1, 1, 2, 3), 2: (1, 2, 3, 4, 5, 6), 3: (1, 1, 2, 2, 3, 4)}[n]
            r_coef = r_msg if n == 1 else ew
            base = stood["src"]
            in_a, in_b, in_c = ph.slots("ed_in_a", ES), ph.slots("ed_in_b", ES), ph.slots("ed_in_c", ES)
            copied, gate, gate_d = ph.slots("ed_copied", ES), ph.sem("ed_gate"), ph.sem("ed_gate_d")
            gate_l = ph.sem("ed_gate_load")
            gat = gathered["src"]
            sems = "turned z_affine z src_product src_relu src_stored affine msg scan rel rel_out dst_affine dst_z"
            tu, za, zz, mm_s, rl_s, sto_s, aff, msg, scn, mm_r, ev_r, da, dz = (ph.slots(f"ed_{x}", ES) for x in sems.split())
            mm_d, rl_d, st_d, sto_d, tr, ev_t, sto_t = (ph.slots(f"ed_{x}", ES) for x in
                                                        "dst_product dst_relu dst_stat dst_stored rows rows_out rows_stored".split())
            ss = ph.sb("ed_same", [C, ES, CW], BF)
            cf = ph.sb("ed_coef", [C, ES, CW])
            xa = ph.sb("ed_xa", [C, ES, kb, CW])
            se = ph.sb("ed_sum", [C, ES, kb, CW])
            hd_in = ph.sb("ed_hd", [C, ES, kb, CW])
            mk = ph.sb("ed_mask", [1, ES, CW], BF)
            ho_d = ph.sb("ed_ho", [C, ES, mb, CW])
            hsi = ph.sb("ed_hs", [C, ES, max(ks, 1), CW])
            zero = ph.sb("ed_zero", [C, 1])
            z0 = ph.sem("ed_zero_set")
            if n == 1:
                rd = ph.sb("ed_rd", [C, ES, CW])
                ag = ph.sb("ed_agg", [C, ES, 1, CW])
            else:
                tg = ph.sb("ed_gathered", [P, ES, EG, ks * C])
                cols = ph.sb("ed_idx", [P, ES, EG], I32)
                ho_s = ph.sb("ed_ho_src", [C, ES, 2, CW])
                stood["src"] += 16 * EG * EI
            if n == 2:
                inv = ph.sb("ed_inv", [C, ES, CW])
                ag = ph.sb("ed_rel", [C, ES, 2, CW])
            if n < 3:
                tb = ph.sb("ed_rows", [P, ES, EG, kb * C])
                tiles = tab[n][0:E, :].rearrange("(t g p) c -> t p g c", p=P, g=EG)
                halves = kb
                hg = EG // halves
            BS, BD, BT, BG = 3, 5, 7, 2
            n_b = 48 if n == 1 else 32
            n_c = 32
            h_src = (hsi, in_a, 16 + 16 * (n == 2)) if n == 1 else (ho_s, rl_s, 2)

            def line(row, k):
                return by_chunk(row)[k].broadcast_to([C, CW])

            def sync(sp):
                def load_source(i, j):
                    k = i * ES + j
                    wait_use(sp, aff[j] if n == 1 else mm_s[j], i - 1, kb if n == 1 else 2)
                    sp.dma_start(hsi[:, j, :, :], hs[max(n - 2, 0)][k]).then_inc(in_a[j], 16)
                    if n == 2:
                        sp.dma_start(inv[:, j, :], line(r_isrc, k)).then_inc(in_a[j], 16)

                def load_rows(i, j):
                    k = i * ES + j
                    if n == 1:
                        wait_use(sp, dz[j], i - 1, 4)
                    else:
                        wait_use(sp, scn[j], i - 1, kb)
                    sp.sem_inc(gate_l, 1)
                    sp.dma_start(ss[:, j, :], line(r_same, k)).then_inc(in_b[j], 16)
                    sp.dma_start(cf[:, j, :], line(r_coef, k)).then_inc(in_b[j], 16)
                    if n == 1:
                        sp.dma_start(rd[:, j, :], line(r_rdst, k)).then_inc(in_b[j], 16)

                def load_dst(i, j):
                    k = i * ES + j
                    wait_use(sp, mm_d[j], i - 1, mb)
                    sp.dma_start(hd_in[:, j, :, :], hd[n - 1][k]).then_inc(in_c[j], 16)
                    sp.dma_start(mk[:, j, :], by_chunk(r_neg_edge)[k]).then_inc(in_c[j], 16)

                return ES, [(max(l_src, l_sum) if n == 1 else l_src, load_source), (l_sum, load_rows), (l_dst, load_dst)], None

            def gpsimd(pool):
                if n == 1:
                    return ES, [], None

                def gather(i, j):
                    wait_use(pool, tu[j], i - 1, ks)
                    pool.sem_inc(gate, 1)
                    pool.tensor_copy(cols[:, j, :], pos_c[:, bass.ds((i * ES + j) * EG, EG)]).then_inc(copied[j], 1)
                    wait_use(pool, copied[j], i)
                    pool.sem_inc(gate, 1)
                    for g in range(EG):
                        pool.indirect_dma_start(tg[:, j, g, :], None, tab[n - 1][:, :],
                                                bass.IndirectOffsetOnAxis(ap=cols[:, j, g:g + 1], axis=0)).then_inc(gat[j], 16)

                return ES, [(0, gather)], None

            def tensor(pe):
                def turn(i, j):
                    wait_use(pe, gat[j], i, 16 * EG, base=base)
                    i1, j1 = before(i, j, 1, ES)
                    wait_use(pe, zz[j1], i1, 2)
                    for g in range(EG):
                        ins = pe.transpose(ps[:, BG, g * P:(g + 1) * P], tg[:, j, g, :], ident[0:P, 0:P])
                    ins.then_inc(tu[j], 1)

                def source(i, j):
                    i1, j1 = before(i, j, 1, ES)
                    if n == 2:
                        wait_use(pe, zz[j], i, 2)
                    else:
                        wait_use(pe, in_a[j], i, 16)
                        wait_use(pe, gat[j], i, 16 * EG, base=base)
                    for m in range(2):
                        wait_use(pe, rl_s[j1], i1, 2, m + 1)
                        o = ps[:, BS + m, 0:CW]
                        if n == 3:
                            for g in range(EG):
                                ins = pe.matmul(ps[:, BS + m, g * P:(g + 1) * P], tg[:, j, g, m * C:(m + 1) * C], ident[0:P, 0:P],
                                                start=g == 0, stop=False, is_transpose=True, skip_group_check=True)
                            ins.then_inc(tu[j], 1)
                        for k in range(ks):
                            w = w1 if n == 2 else wfold[2]
                            ins = pe.matmul(o, w[:, k, m * C:(m + 1) * C], hsi[:, j, k, :],
                                            start=n == 2 and k == 0, stop=k == ks - 1, skip_group_check=n == 3)
                        ins.then_inc(mm_s[j], 1)

                def rel(i, j):
                    i1, j1 = before(i, j, 1, ES)
                    for m in range(mb):
                        wait_use(pe, rl_d[j1], i1, mb, m + 1)
                        for k in range(kb):
                            wait_use(pe, scn[j], i, kb, k + 1)
                            ins = pe.matmul(ps[:, BD + m, 0:CW], wrel[n][:, k, m * C:(m + 1) * C], se[:, j, k, :],
                                            start=k == 0, stop=k == kb - 1)
                        ins.then_inc(mm_r[j], 1)

                def dst(i, j):
                    i1, j1 = before(i, j, 1, ES)
                    wait_use(pe, in_c[j], i, n_c)
                    if n == 1:
                        wait_use(pe, dz[j], i, 4)
                    if n == 3:
                        wait_use(pe, scn[j], i, kb)
                    for m in range(mb):
                        mc = slice(m * C, (m + 1) * C)
                        if n == 2:
                            wait_use(pe, ev_r[j], i, 2, m + 1)
                        else:
                            wait_use(pe, rl_d[j1], i1, mb, m + 1)
                        o = ps[:, BD + m, 0:CW]
                        pe.matmul(o, ones_row[:, :], mk[:, j, :], start=n != 2, stop=False, skip_group_check=n == 2)
                        terms = [((w1 if n == 1 else wfold[n])[:, k, mc], hd_in[:, j, k, :]) for k in range(kb)]
                        if n == 3:
                            terms += [(wrel[n][:, k, mc], se[:, j, k, :]) for k in range(kb)]
                        for t, (a, b) in enumerate(terms):
                            ins = pe.matmul(o, a, b, start=False, stop=t == len(terms) - 1, skip_group_check=n == 2)
                        ins.then_inc(mm_d[j], 1)

                def table(half):
                    def turn_rows(i, j):
                        if half == 0:
                            i1, j1 = before(i, j, 1, ES)
                            wait_use(pe, ev_t[j1], i1, halves)
                            if n == 1:
                                wait_use(pe, dz[j], i, 4, 1)
                            else:
                                wait_use(pe, ev_r[j], i, 2)
                        else:
                            wait_use(pe, ev_t[j], i, halves, half)
                        for g in range(hg):
                            for k in range(kb):
                                e = (half * hg + g) * P
                                ins = pe.transpose(ps[0:P, BT, (g * kb + k) * C:(g * kb + k + 1) * C], ag[:, j, k, e:e + P], ident[:, :])
                        ins.then_inc(tr[j], 1)

                    return turn_rows

                stages = [(l_dst, table(0))] if n < 3 else []
                stages += [(l_dst, dst)]
                stages += [(l_dst, table(1))] if n == 2 else []
                stages += [(l_turn, turn)] if n == 2 else []
                stages += [(l_src, source)] if n > 1 else []
                stages += [(l_rel, rel)] if n == 2 else []
                return ES, stages, None

            def vector(dve):
                dve.memset(zero[:, :], 0.0).then_inc(z0, 1)
                dve.wait_ge(z0, 1)

                def source_z(i, j):
                    wait_use(dve, in_a[j], i, 32)
                    wait_use(dve, za[j], i)
                    dve.tensor_tensor(hsi[:, j, 0, :], hsi[:, j, 0, :], inv[:, j, :], ALU.mult).then_inc(zz[j], 1)
                    wait_use(dve, zz[j], i, 2, 1)
                    wait_use(dve, tu[j], i)
                    dve.tensor_tensor(hsi[:, j, 0, :], hsi[:, j, 0, :], ps[:, BG, 0:CW], ALU.add).then_inc(zz[j], 1)

                def sums(i, j):
                    wait_use(dve, in_b[j], i, n_b)
                    for k in range(kb):
                        wait_use(dve, aff[j], i, kb, k + 1)
                        dve.tensor_tensor(xa[:, j, k, :], xa[:, j, k, :], cf[:, j, :], ALU.mult).then_inc(msg[j], 1)
                    if n == 1:
                        wait_use(dve, dz[j], i - 1, 4)
                    elif n == 2:
                        wait_use(dve, mm_r[j], i - 1, mb)
                    else:
                        wait_use(dve, mm_d[j], i - 1, mb)
                    i1, j1 = before(i, j, 1, ES)
                    wait_use(dve, scn[j1], i1, kb)
                    for k in range(kb):
                        wait_use(dve, msg[j], i, kb, k + 1)
                        fresh = isinstance(i1, int) and i1 < 0
                        start = zero[:, 0:1] if fresh else se[:, j1, k, CW - 1:CW]
                        dve.tensor_tensor_scan(se[:, j, k, :], ss[:, j, :], xa[:, j, k, :], start, ALU.mult, ALU.add).then_inc(scn[j], 1)
                    if n == 1:
                        wait_use(dve, scn[j], i)
                        wait_use(dve, tr[j], i - 1)
                        dve.tensor_tensor(ag[:, j, 0, :], se[:, j, 0, :], rd[:, j, :], ALU.mult).then_inc(dz[j], 1)
                        wait_use(dve, da[j], i)
                        dve.tensor_tensor(hd_in[:, j, 0, :], hd_in[:, j, 0, :], rd[:, j, :], ALU.mult).then_inc(dz[j], 1)
                        wait_use(dve, dz[j], i, 4, 2)
                        dve.tensor_tensor(hd_in[:, j, 0, :], hd_in[:, j, 0, :], se[:, j, 0, :], ALU.add).then_inc(dz[j], 1)
                        wait_use(dve, dz[j], i, 4, 3)
                        dve.tensor_tensor(hd_in[:, j, 0, :], hd_in[:, j, 0, :], rd[:, j, :], ALU.mult).then_inc(dz[j], 1)

                def statistics(i, j):
                    for m in range(mb):
                        wait_use(dve, rl_d[j], i, mb, m + 1)
                        dve.sem_inc(gate_d, 1)
                        dve.bn_stats(stats[:, m, NT * CH + i * ES + j, :], ho_d[:, j, m, :]).then_inc(st_d[j], 1)

                stages = [(l_dst, statistics)]
                stages += [(l_turn, source_z)] if n == 2 else []
                stages += [(l_sum, sums)]
                return ES, stages[::-1] if n == 1 else stages, None

            def scalar(act):
                def store_source(i, j):
                    wait_use(act, rl_s[j], i, 2)
                    act.dma_start(hs[1][i * ES + j], ho_s[:, j, :, :]).then_inc(sto_s[j], 16)

                def store_dst(i, j):
                    wait_use(act, rl_d[j], i, mb)
                    act.dma_start(hd[n][i * ES + j], ho_d[:, j, :, :]).then_inc(sto_d[j], 16)

                def store_table(i, j):
                    wait_use(act, ev_t[j], i, halves)
                    act.dma_start(tiles[i * ES + j], tb[:, j, :, :]).then_inc(sto_t[j], 16)

                def end():
                    for j in range(ES):
                        act.wait_ge(sto_d[j], 16 * EI)
                        if n < 3:
                            act.wait_ge(sto_t[j], 16 * EI)
                        if n == 2:
                            act.wait_ge(sto_s[j], 16 * EI)

                def source_affine(i, j):
                    wait_use(act, in_a[j], i, 32)
                    act.activation(hsi[:, j, 0, :], hsi[:, j, 0, :], ACT.Identity, bias=sft[0][:, 0:1], scale=sca[0][:, 0:1]).then_inc(za[j], 1)

                def source_relu(i, j):
                    wait_use(act, aff[j], i - 1, kb)
                    if n == 2:
                        wait_use(act, sto_s[j], i - 1, 16)
                    for m in range(2):
                        wait_use(act, mm_s[j], i, 2, m + 1)
                        b = bias[1] if n == 2 else bfold[2]
                        act.activation(ho_s[:, j, m, :], ps[:, BS + m, 0:CW], ACT.Relu, bias=b[:, m:m + 1]).then_inc(rl_s[j], 1)

                def affine(i, j):
                    src_t, src_sem, src_n = h_src
                    wait_use(act, scn[j], i - 1, kb)
                    for k in range(kb):
                        wait_use(act, src_sem[j], i, src_n, src_n if n == 1 else k + 1)
                        act.activation(xa[:, j, k, :], src_t[:, j, k, :], ACT.Identity, bias=sft[n - 1][:, k:k + 1],
                                       scale=sca[n - 1][:, k:k + 1]).then_inc(aff[j], 1)
                    if n == 1:
                        wait_use(act, in_c[j], i, n_c)
                        act.activation(hd_in[:, j, 0, :], hd_in[:, j, 0, :], ACT.Identity, bias=sft[0][:, 0:1],
                                       scale=sca[0][:, 0:1]).then_inc(da[j], 1)

                def rel_out(i, j):
                    wait_use(act, tr[j], i - 1, halves)
                    for m in range(2):
                        wait_use(act, mm_r[j], i, 2, m + 1)
                        act.activation(ag[:, j, m, :], ps[:, BD + m, 0:CW], ACT.Copy).then_inc(ev_r[j], 1)

                def table_out(half):
                    def rows_out(i, j):
                        if half == 0:
                            wait_use(act, sto_t[j], i - 1, 16)
                        wait_use(act, tr[j], i, halves, half + 1)
                        act.activation(tb[:, j, half * hg:(half + 1) * hg, :],
                                       ps[0:P, BT, 0:hg * kb * C].rearrange("p (g c) -> p g c", g=hg), ACT.Copy).then_inc(ev_t[j], 1)

                    return rows_out

                def dst_relu(i, j):
                    wait_use(act, sto_d[j], i - 1, 16)
                    wait_use(act, st_d[j], i - 1, mb)
                    b = bias[1] if n == 1 else bfold[n]
                    for m in range(mb):
                        wait_use(act, mm_d[j], i, mb, m + 1)
                        act.activation(ho_d[:, j, m, :], ps[:, BD + m, 0:CW], ACT.Relu, bias=b[:, m:m + 1]).then_inc(rl_d[j], 1)

                stages = [(l_dst, table_out(0))] if n < 3 else []
                stages += [(l_dst, dst_relu)]
                stages += [(l_dst, table_out(1))] if n == 2 else []
                stages += [(l_turn, source_affine)] if n == 2 else []
                stages += [(l_src, source_relu)] if n > 1 else []
                stages += [(l_src if n > 1 else l_sum, affine)]
                stages += [(l_rel, rel_out)] if n == 2 else []
                stages += [(l_src + 1, store_source)] if n == 2 else []
                stages += [(l_out, store_table)] if n < 3 else []
                if n == 1:
                    stages = stages[-2:-1] + stages[:-2] + stages[-1:]
                return ES, stages + [(l_out, store_dst)], end

            return dict(sync=sync, gpsimd=gpsimd, tensor=tensor, vector=vector, scalar=scalar)

        def fold(n, blocks, groups, weight, folded, b_in, b_out, masks=False):
            ratio = groups * CW / N
            with Phase(nc, f"fold{n}") as ph:
                s, pwd, pd = ph.sem("steps"), ph.sem("pow"), ph.sem("bias")
                mv = ph.sb("mv", [C, blocks, 2])
                t1, t2, t3 = (ph.sb(f"t{k}", [C, blocks]) for k in (1, 2, 3))
                ps = ph.pb("ps", 2)
                if masks:
                    node_in, nd, npe = ph.sem("node_in"), ph.sem("node_dve"), ph.sem("node_pe")
                    node_out = ph.slots("node_out", 2)
                    flags = ph.sb("flags", [P, NT * G])
                    nmap = ph.sb("nmap", [P, NT, 2 * G])
                    nrow = ph.sb("neg_rows", [128, 2, P], BF)
                    pm = ph.pb("pm", 2)
                    blocks_m = [(128 * b, min(128, NT * G - 128 * b)) for b in range(-(-(NT * G) // 128))]
                block = ph.start()

                @block.sync
                def _(sp):
                    if not masks:
                        return
                    sp.dma_start(nmap[:, :, :], node_map[0:N, :].rearrange("(t p g) c -> p t (g c)", p=P, g=G)).then_inc(node_in, 16)
                    for b, (at, width) in enumerate(blocks_m):
                        sp.wait_ge(nd, b + 2)
                        sp.dma_start(r_neg_node[at:at + width, :], nrow[0:width, b % 2, :]).then_inc(node_out[b % 2], 16)
                    for j in range(min(2, len(blocks_m))):
                        sp.wait_ge(node_out[j], 16 * ((len(blocks_m) - j + 1) // 2))

                @block.vector
                def _(dve):
                    done = [0]

                    def link(ins):
                        done[0] += 1
                        ins.then_inc(s, 1)
                        dve.wait_ge(s, done[0])

                    if masks:
                        dve.wait_ge(node_in, 16)
                        dve.tensor_scalar(flags[:, :].rearrange("p (t g) -> p t g", g=G),
                                          nmap[:, :, :].rearrange("p t (g c) -> p t g c", c=2)[:, :, :, 0],
                                          float(E), None, ALU.is_lt).then_inc(nd, 1)
                        for b, (at, width) in enumerate(blocks_m):
                            dve.wait_ge(npe, b + 1)
                            if b >= 2:
                                dve.wait_ge(node_out[b % 2], 16 * (b // 2))
                            dve.tensor_scalar(nrow[0:width, b % 2, :], pm[0:width, b % 2, 0:P], MASK, None, ALU.mult).then_inc(nd, 1)
                    for b in range(blocks):
                        link(dve.bn_aggr(mv[:, b, :], stats[:, b, 0:groups, :].rearrange("p g s -> p (g s)")))
                    mean, var = mv[:, :, 0], mv[:, :, 1]
                    link(dve.tensor_tensor(t1[:, :], mean, mean, ALU.mult))
                    link(dve.tensor_tensor(t2[:, :], var, t1[:, :], ALU.add))
                    link(dve.tensor_scalar(t2[:, :], t2[:, :], ratio, None, ALU.mult))
                    link(dve.tensor_scalar(t1[:, :], mean, ratio, None, ALU.mult))
                    link(dve.tensor_tensor(t3[:, :], t1[:, :], t1[:, :], ALU.mult))
                    link(dve.tensor_tensor(t2[:, :], t2[:, :], t3[:, :], ALU.subtract))
                    link(dve.tensor_scalar(t2[:, :], t2[:, :], 0.0, EPS, ALU.max, ALU.add))
                    dve.wait_ge(pwd, 1)
                    link(dve.tensor_tensor(sca[n][:, :], gam[n][:, :], t3[:, :], ALU.mult))
                    link(dve.tensor_tensor(t1[:, :], t1[:, :], sca[n][:, :], ALU.mult))
                    link(dve.tensor_tensor(sft[n][:, :], bet[n][:, :], t1[:, :], ALU.subtract))
                    if weight is None:
                        return
                    for k in range(blocks):
                        link(dve.tensor_scalar(folded[:, k, :], weight[:, k, :], sca[n][:, k:k + 1], None, ALU.mult))
                    for m in range(b_in.shape[1]):
                        dve.wait_ge(pd, m + 1)
                        link(dve.tensor_tensor(b_out[:, m:m + 1], b_in[:, m:m + 1], ps[:, m, 0:1], ALU.add))

                @block.gpsimd
                def _(pool):
                    pool.wait_ge(s, blocks + 7)
                    pool.tensor_tensor(t3[:, :], t2[:, :], mhalf[:, 0:blocks], ALU.pow).then_inc(pwd, 1)

                @block.tensor
                def _(pe):
                    if masks:
                        pe.wait_ge(nd, 1)
                        for b, (at, width) in enumerate(blocks_m):
                            if b >= 2:
                                pe.wait_ge(nd, b)
                            pe.matmul(pm[0:width, b % 2, 0:P], flags[:, at:at + width], ident[0:P, 0:P],
                                      start=True, stop=True).then_inc(npe, 1)
                    if weight is None:
                        return
                    pe.wait_ge(s, blocks + 10)
                    for m in range(b_in.shape[1]):
                        for k in range(blocks):
                            ins = pe.matmul(ps[:, m, 0:1], weight[:, k, m * C:(m + 1) * C], sft[n][:, k:k + 1],
                                            start=k == 0, stop=k == blocks - 1)
                        ins.then_inc(pd, 1)

        def source_rows():
            with Phase(nc, "sources") as ph:
                rows, pw, steps = ph.sem("rows"), ph.sem("pow"), ph.sem("steps")
                rsrc, isrc, cmsg = ph.sb("rsrc", [P, ET]), ph.sb("isrc", [P, ET]), ph.sb("cmsg", [P, ET])
                posi = ph.sb("posi", [P, ET], I32)
                block = ph.start()

                @block.gpsimd
                def _(pool):
                    pool.tensor_tensor(rsrc[:, :], msrc[:, :, 1], mhalf[0:P, 0:ET], ALU.pow).then_inc(pw, 1)

                @block.vector
                def _(dve):
                    dve.tensor_copy(posi[:, :], msrc[:, :, 0]).then_inc(steps, 1)
                    dve.reciprocal(isrc[:, :], msrc[:, :, 1]).then_inc(steps, 1)
                    dve.wait_ge(pw, 1)
                    dve.tensor_tensor(cmsg[:, :], w_b[:, :], rsrc[:, :], ALU.mult).then_inc(steps, 1)

                @block.sync
                def _(sp):
                    flat = lambda r: r.rearrange("(p t) -> p t", t=ET)
                    sp.wait_ge(steps, 1)
                    sp.dma_start(flat(r_pos), posi[:, :]).then_inc(rows, 16)
                    sp.wait_ge(rows, 16)
                    sp.dma_start(pos_c[:, :], r_pos.rearrange("(t p) -> p t", p=P), allow_slow_non_contiguous=True).then_inc(rows, 16)
                    sp.wait_ge(steps, 3)
                    sp.dma_start(flat(r_msg), cmsg[:, :]).then_inc(rows, 16)
                    sp.dma_start(flat(r_isrc), isrc[:, :]).then_inc(rows, 16)
                    sp.wait_ge(rows, 64)

        def output(ph, name, slots, groups, bank0, ps):
            dense = name == "od"
            banks = max(groups // EG, 1)
            gb = groups // banks
            rounds = DI if dense else EI
            h_in = h3 if dense else hd[3]
            got, gx, cpd, gate = ph.slots(f"{name}_in", slots), ph.slots(f"{name}_x", slots) if dense else gathered["x"], ph.slots(f"{name}_copied", slots), ph.sem(f"{name}_gate")
            aff, tr, sm, sto = (ph.slots(f"{name}_{n}", slots) for n in ("affine", "turned", "summed", "stored"))
            hi = ph.sb(f"{name}_hi", [C, slots, groups * P])
            xt = ph.sb(f"{name}_xt", [P, slots, groups, C])
            ot = ph.sb(f"{name}_ot", [P, slots, groups, C]) if dense else None
            cols = ph.sb(f"{name}_idx", [P, slots, groups], I32)
            out_rows = out[0:N, :].rearrange("(t p g) c -> t p g c", p=P, g=G)
            l_turn, l_add = (0, 0) if dense else (1, 2)

            def sync(sp):
                def load(i, j):
                    k = i * slots + j
                    wait_use(sp, tr[j], i - 1, banks)
                    h = h_in[k] if dense else h_in[i * ES + j // 2][:, :, j % 2 * QG * P:(j % 2 + 1) * QG * P]
                    sp.dma_start(hi[:, j, :], h.rearrange("c a w -> c (a w)")).then_inc(got[j], 16)
                    if dense:
                        wait_use(sp, sm[j], i - 1, banks)
                        sp.dma_start(xt[0:120, j, :, :], x_tiles[k, 0:120]).then_inc(gx[j], 16)
                        sp.dma_start(xt[120:P, j, :, :], x_tiles[k, 120:P]).then_inc(gx[j], 16)

                def store(i, j):
                    k = i * slots + j
                    wait_use(sp, sm[j], i, banks)
                    sp.dma_start(out_rows[k, 0:120], ot[0:120, j, :, :]).then_inc(sto[j], 16)
                    sp.dma_start(out_rows[k, 120:P], ot[120:P, j, :, :]).then_inc(sto[j], 16)

                def end():
                    for j in range(slots):
                        sp.wait_ge(sto[j], 32 * rounds)
                    sp.sem_inc(out_written, 1)

                return slots, [(0 if dense else l_turn, load)] + ([(slots - 1, store)] if dense else []), end if dense else None

            def gpsimd(pool):
                def gather(i, j):
                    wait_use(pool, sm[j], i - 1)
                    pool.sem_inc(gate, 1)
                    pool.tensor_copy(cols[:, j, :], dst_c[:, bass.ds((i * slots + j) * groups, groups)]).then_inc(cpd[j], 1)
                    wait_use(pool, cpd[j], i)
                    pool.sem_inc(gate, 1)
                    for g in range(groups):
                        pool.indirect_dma_start(xt[:, j, g, :], None, x[:, :],
                                                bass.IndirectOffsetOnAxis(ap=cols[:, j, g:g + 1], axis=0)).then_inc(gx[j], 16)

                def end():
                    pool.wait_ge(out_written, 1)
                    for j in range(slots):
                        pool.wait_ge(sm[j], rounds)
                    for t in range(ET):
                        pool.indirect_dma_start(out[:, :], bass.IndirectOffsetOnAxis(ap=out_c[:, t:t + 1], axis=0),
                                                rows_dst[:, t, :], None).then_inc(gathered["out"][0], 16)
                    pool.wait_ge(gathered["out"][0], 16 * ET)

                return slots, [] if dense else [(0, gather)], None if dense else end

            def scalar(act):
                def affine(i, j):
                    wait_use(act, got[j], i, 16)
                    act.activation(hi[:, j, :], hi[:, j, :], ACT.Identity, bias=sft[3][:, 0:1], scale=sca[3][:, 0:1]).then_inc(aff[j], 1)

                return slots, [(l_turn, affine)], None

            def tensor(pe):
                def turn(i, j):
                    wait_use(pe, aff[j], i)
                    i2, j2 = before(i, j, 2, slots)
                    wait_use(pe, sm[j2], i2, banks)
                    for b in range(banks):
                        for g in range(gb):
                            e = (b * gb + g) * P
                            ins = pe.transpose(ps[0:P, bank0 + (j % 2) * banks + b, g * C:(g + 1) * C], hi[:, j, e:e + P], ident[:, :])
                        ins.then_inc(tr[j], 1)

                return slots, [(l_turn, turn)], None

            def vector(dve):
                def add(i, j):
                    wait_use(dve, gx[j], i, 32 if dense else 16 * groups)
                    if dense:
                        wait_use(dve, sto[j], i - 1, 32)
                    for b in range(banks):
                        wait_use(dve, tr[j], i, banks, b + 1)
                        part = slice(b * gb, (b + 1) * gb)
                        rows = ot[:, j, part, :] if dense else rows_dst[:, bass.ds((i * slots + j) * groups, groups), :]
                        dve.tensor_tensor(rows, ps[0:P, bank0 + (j % 2) * banks + b, 0:gb * C].rearrange("p (g c) -> p g c", g=gb),
                                          xt[:, j, part, :], ALU.add).then_inc(sm[j], 1)

                return slots, [(l_add, add)], None

            return dict(sync=sync, gpsimd=gpsimd, scalar=scalar, tensor=tensor, vector=vector)

        with Phase(nc, "norm") as ph:
            ps = ph.pb("ps", 6)
            side_by_side(ph, DI, [layer_norm(ph, "ln_dense", NS, G, None, h0, (ps, 0, 2), True),
                                  layer_norm(ph, "ln_src", QS, QG, src_c, hs[0], (ps, 4, 2), False),
                                  map_scatter(ph)])
        fold(0, 1, NT * CH, w1, wfold[1], bias[1], bfold[1], masks=True)
        with Phase(nc, "l1") as ph:
            ps = ph.pb("ps", 6)
            side_by_side(ph, DI, [dense_layer(ph, 1, 1, 2, h0, h1, ps),
                                  layer_norm(ph, "ln_dst", QS, QG, dst_c, hd[0], (ps, 4, 2), False),
                                  map_gather(ph)])
        source_rows()
        with Phase(nc, "l1_edges") as ph:
            side_by_side(ph, EI, [edge_layer(ph, 1, ph.pb("ps", 8))])
        fold(1, 2, BN, wroot[2], wfold[2], bias[2], bfold[2])
        with Phase(nc, "l2") as ph:
            ps = ph.pb("ps", 8)
            side_by_side(ph, DI, [dense_layer(ph, 2, 2, 2, h1, h2, ps), edge_layer(ph, 2, ps)])
        fold(2, 2, BN, wroot[3], wfold[3], bias[3], bfold[3])
        with Phase(nc, "l3") as ph:
            ps = ph.pb("ps", 8)
            side_by_side(ph, DI, [dense_layer(ph, 3, 2, 1, h2, h3, ps), edge_layer(ph, 3, ps)])
        fold(3, 1, BN, None, None, None, None)
        with Phase(nc, "out") as ph:
            ps = ph.pb("ps", 6)
            rows_dst = ph.sb("rows_dst", [P, ET, C])
            out_written = ph.sem("dense_written")
            side_by_side(ph, DI, [output(ph, "od", NS, G, 0, ps), output(ph, "oe", QS, QG, 4, ps)])


def kernel(**inputs):
    import numpy as np
    import concourse.bacc as bacc
    from concourse.bass_utils import run_bass_kernel_spmd as run

    nc = bacc.Bacc("TRN2", target_bir_lowering=False, num_devices=1)
    arrays, aps = {}, {}
    for name in inputs:
        a = np.ascontiguousarray(inputs[name])
        arrays["in_" + name] = a
        aps[name] = nc.dram_tensor("in_" + name, a.shape, mybir.dt.from_np(a.dtype), kind="ExternalInput").ap()
    n, e = inputs["x"].shape[0], inputs["src"].shape[0]
    out = nc.dram_tensor("out", (n + e, C), FP, kind="ExternalOutput").ap()
    prm = {name[len("L0_gnn_"):]: aps[name] for name in inputs if name.startswith("L0_gnn_")}
    build(nc, aps["x"], aps["src"], aps["dst"], aps["edge_weight"], prm, out)
    r = run(nc, [arrays], core_ids=[0])
    return r.results[0]["out"][:n]
```

```python
from contextlib import ExitStack

import concourse.bass as bass
from concourse import mybir

FP = mybir.dt.float32
FR = mybir.dt.float32r
BF = mybir.dt.bfloat16
I32 = mybir.dt.int32
ALU = mybir.AluOpType
ACT = mybir.ActivationFunctionType

P = 125
C = 128
G = 8
W = P * G
EG = 4
CW = P * EG
CH = W // CW
NS = 4
ES = 2
QS = 4
QG = EG // 2
TOP_BITS = -4096
RSQRT_SEED = 0x5f3759df
EPS = 1e-5
MASK = -3.0e38


class Phase:

    def __init__(self, nc, name):
        self.nc, self.name, self.memory, self.sems = nc, name, ExitStack(), []

    def __enter__(self):
        return self

    def sb(self, name, shape, dt=FP):
        return self.memory.enter_context(self.nc.sbuf_tensor(f"{self.name}_{name}", shape, dt))

    def pb(self, name, banks):
        return self.memory.enter_context(self.nc.psum_tensor(f"{self.name}_{name}", [128, banks, 512], FP))

    def sem(self, name):
        s = self.memory.enter_context(self.nc.semaphore(f"{self.name}_{name}"))
        self.sems.append(s)
        return s

    def slots(self, name, n):
        return [self.sem(f"{name}{j}") for j in range(n)]

    def start(self):
        self.ctx = self.nc.Block()
        return self.ctx.__enter__()

    def __exit__(self, kind, *rest):
        if kind is None:
            self.ctx.__exit__(None, None, None)
            if self.sems:
                with self.nc.Block() as block:
                    @block.gpsimd
                    def _(pool):
                        for s in self.sems:
                            pool.sem_clear(s)
            self.memory.close()
        return False


def wait_use(eng, sem, i, per=1, upto=None, base=0):
    if isinstance(i, int) and i < 0:
        return
    eng.wait_ge(sem, i * per + (base + (per if upto is None else upto)))


def pipeline(eng, rounds, streams):
    streams = [x for x in streams if x[1]]
    if not streams:
        return
    most = max(slots for slots, _ in streams)
    extra = max(-(-lag // slots) for slots, stages in streams for lag, _ in stages)

    def round_(i):
        for turn in range(most):
            for slots, stages in streams:
                if (turn + 1) * slots % most:
                    continue
                j = (turn + 1) * slots // most - 1
                for lag, step in stages:
                    at, slot = before(i, j, lag, slots)
                    if not isinstance(at, int) or 0 <= at < rounds:
                        step(at, slot)

    peeled = min(extra + 1, rounds)
    for i in range(peeled):
        round_(i)
    if peeled < rounds:
        with eng.Fori(peeled, rounds) as i:
            round_(i)
    for i in range(rounds, rounds + extra):
        round_(i)


def side_by_side(ph, rounds, works):
    block = ph.start()

    def run(eng, name):
        parts = [w[name](eng) for w in works if name in w]
        if parts:
            pipeline(eng, rounds, [(slots, stages) for slots, stages, _ in parts])
            for _, _, end in parts:
                if end:
                    end()

    @block.sync
    def _(sp):
        run(sp, "sync")

    @block.gpsimd
    def _(pool):
        run(pool, "gpsimd")

    @block.scalar
    def _(act):
        run(act, "scalar")

    @block.tensor
    def _(pe):
        run(pe, "tensor")

    @block.vector
    def _(dve):
        run(dve, "vector")


def before(i, j, d, slots):
    return i - (d - j + slots - 1) // slots if d > j else i, (j - d) % slots


def build(nc, x, src, dst, ew, prm, out):
    N, E = x.shape[0], src.shape[0]
    NT = N // W
    EC = E // CW
    ET = E // P
    TB = -(-ET // 128)
    TR = ET // TB
    tile_rows = lambda row: row.rearrange("(b t p) -> t b p", b=TB, p=P)
    DI, EI = NT // NS, EC // ES
    assert N == DI * NS * W and ET == TB * TR and E == EI * ES * CW and DI > 1 and EI > 1
    E1S = next(n for n in (5, 4, 3, 2) if EC % n == 0)
    H1 = prm["W1"].shape[1]
    BN = NT * CH + EC

    def dram(name, shape, dt=FP):
        return nc.dram_tensor(name, shape, dt, kind="Internal").ap()

    h0 = dram("h0_dense", (NT, C, 1, W))
    h1 = dram("h1_dense", (NT, C, 2, W))
    h2 = dram("h2_dense", (NT, C, 2, W))
    h3 = dram("h3_dense", (NT, C, 1, W))
    hs = [dram(f"h{n}_src", (EC, C, k, CW)) for n, k in ((0, 1), (1, 2), (2, 2))]
    hd = [dram(f"h{n}_dst", (EC, C, k, CW)) for n, k in ((0, 1), (1, 2), (2, 2), (3, 1))]
    tab = [None] + [dram(f"agg_rows{n}", (E + P, k * C)) for n, k in ((1, 1), (2, 2))]
    x_dst = dram("x_dst", (E // P // QG, P, QG, C))
    node_map = dram("node_map", (N + E, 2))
    r_same = dram("row_same", (E,), BF)
    r_msg = dram("row_msg", (E,))
    r_isrc = dram("row_inv_deg_src", (E,))
    r_rdst = dram("row_rsqrt_deg_dst", (E,))
    r_neg_edge = dram("row_neg_edge", (E,), BF)
    r_neg_node = dram("row_neg_node", (NT * G, P), BF)
    r_pos = dram("row_pos_src", (E,), I32)
    r_out = dram("row_out_node", (E,), I32)

    keep = ExitStack()
    with keep:
        def sb(name, shape, dt=FP):
            return keep.enter_context(nc.sbuf_tensor(name, shape, dt))

        ident = sb("ident", [128, 128])
        ones_row = sb("ones_row", [1, 128], BF)
        zero_row = sb("zero_row", [P, 2 * C])
        w1 = sb("w1", [C, 1, H1])
        wroot = [None, None, None, sb("wroot3", [C, 2, C])]
        wrel = [None, None, sb("wrel2", [C, 2, H1]), sb("wrel3", [C, 2, C])]
        wfold = [None, None, sb("wroot2_fold", [C, 2, H1]), sb("wroot3_fold", [C, 2, C])]
        wparts = [sb(f"wroot2_{n}", [C, 2, H1], FR) for n in ("top", "rest")]
        bias = [None] + [sb(f"bias{n}", [C, k]) for n, k in ((1, 2), (2, 2), (3, 1))]
        bfold = [None] + [sb(f"bias{n}_fold", [C, k]) for n, k in ((1, 2), (2, 2), (3, 1))]
        gam = [sb(f"gamma{n}", [C, k]) for n, k in enumerate((1, 2, 2, 1))]
        bet = [sb(f"beta{n}", [C, k]) for n, k in enumerate((1, 2, 2, 1))]
        sca = [sb(f"bn_scale{n}", [C, k]) for n, k in enumerate((1, 2, 2, 1))]
        sft = [sb(f"bn_shift{n}", [C, k]) for n, k in enumerate((1, 2, 2, 1))]
        stats = sb("bn_stats_all", [C, 2, BN, 6])
        pos_c = sb("pos_cols", [P, ET], I32)
        out_c = sb("out_cols", [P, ET], I32)
        rounds_first = sb("rounds_first", [1, EI], I32)
        mhalf = sb("minus_half", [128, G])
        front = keep.enter_context(ExitStack())

        def front_sb(name, shape, dt=FP):
            return front.enter_context(nc.sbuf_tensor(name, shape, dt))

        wroot[2], wfold[1] = front_sb("wroot2", [C, 2, H1]), front_sb("w1_fold", [C, 1, H1])
        mval = front_sb("map_values", [P, ET, 2])
        sidx = front_sb("scatter_idx", [P, ET], I32)
        s_b = front_sb("src_b", [P, ET], I32)
        w_b = front_sb("ew_b", [P, ET])
        src_c = front_sb("src_cols", [P, ET], I32)
        dst_c = front_sb("dst_cols", [P, ET], I32)
        msrc = front_sb("map_src", [P, ET, 2])
        gathered = {key: [keep.enter_context(nc.semaphore(f"sw_{key}{j}")) for j in range(QS)]
                    for key in ("ln", "map_out", "map_in", "src", "out")}
        stood = {"ln": 0, "src": 0}

        with Phase(nc, "setup") as ph:
            wl, cst = ph.sem("weights_in"), ph.sem("constants")
            edge_in, fill = ph.sem("edges_in"), ph.sem("filled")
            ds, ps_, ob = ph.sem("dve_steps"), ph.sem("pe_steps"), ph.sem("rows_out")
            last_in = ph.sem("last_nodes_in")
            d_b = ph.sb("dst_b", [P, ET], I32)
            dp_b = ph.sb("dst_prev", [P, ET], I32)
            dn_b = ph.sb("dst_next", [P, ET], I32)
            pos_i = ph.sb("pos_i", [P, ET], I32)
            same = ph.sb("same", [P, ET])
            zeros = ph.sb("zeros", [P, ET])
            pa = ph.sb("prefix_all", [P, ET])
            sc = ph.sb("segsum", [P, ET])
            arow, brow = ph.sb("arow", [1, P]), ph.sb("brow", [1, P])
            crow = ph.sb("crow", [1, P + 1])
            carry = ph.sb("carry", [P, 1])
            last = ph.sb("last", [P, ET])
            pos_n = ph.sb("pos_n", [P, ET])
            dif = ph.sb("dif", [P, ET])
            neg = ph.sb("neg_edge", [P, ET], BF)
            deg, root, halves = (ph.sb(n, [P, ET]) for n in ("degree", "rsqrt_degree", "halves"))
            last_node, last_f, count = ph.sb("last_node", [1, EI], I32), ph.sb("last_node_f", [1, EI]), ph.sb("rounds", [1, EI])
            same_row = ph.sb("same_row", [P, ET], BF)
            blank = ph.sb("map_blank", [P, N // P, 2])
            pst = ph.pb("ps", 1)
            pst2 = ph.pb("ps2", 1)
            pst3 = ph.pb("ps3", 1)
            pst4 = ph.pb("ps4", 3)
            rows_i, rows_f = ph.sb("rows_i", [TR, 3, TB, P], I32), ph.sb("rows_f", [TR, 3, TB, P])
            rows_in, rows_ready, turned = ph.sem("rows_in"), ph.sem("rows_ready"), ph.sem("turned")
            block = ph.start()

            @block.sync
            def _(sp):
                sp.dma_start(s_b[:, :], src.rearrange("(p t) -> p t", t=ET)).then_inc(edge_in, 16)
                sp.dma_start(d_b[:, :], dst.rearrange("(p t) -> p t", t=ET)).then_inc(edge_in, 16)
                sp.dma_start(w_b[:, :], ew.rearrange("(p t) -> p t", t=ET)).then_inc(edge_in, 16)
                sp.wait_ge(fill, 2)
                sp.dma_start(dp_b[0:1, 1:ET], dst[0:ET - 1].rearrange("(a t) -> a t", a=1)).then_inc(edge_in, 16)
                sp.dma_start(dp_b[1:P, :], dst[ET - 1:E - 1].rearrange("(p t) -> p t", t=ET)).then_inc(edge_in, 16)
                sp.dma_start(dn_b[0:P - 1, :], dst[1:E - ET + 1].rearrange("(p t) -> p t", t=ET)).then_inc(edge_in, 16)
                sp.dma_start(dn_b[P - 1:P, 0:ET - 1], dst[E - ET + 1:E].rearrange("(a t) -> a t", a=1)).then_inc(edge_in, 16)
                sp.dma_start(rows_i[:, 0, :, :], tile_rows(src)).then_inc(rows_in, 16)
                sp.dma_start(rows_i[:, 1, :, :], tile_rows(dst)).then_inc(rows_in, 16)
                sp.dma_start(w1[:, 0, :], prm["W1"]).then_inc(wl, 16)
                for t, name in ((wroot[2], "Wroot2"), (wroot[3], "Wroot3"), (wrel[2], "Wrel2"), (wrel[3], "Wrel3")):
                    sp.dma_start(t[:, :, :], prm[name].rearrange("(k p) n -> p k n", p=C)).then_inc(wl, 16)
                vectors = [(bias[1], "b1"), (bias[2], "brel2"), (bias[3], "brel3")]
                vectors += [(gam[n], f"g{n}") for n in range(4)] + [(bet[n], f"be{n}") for n in range(4)]
                for t, name in vectors:
                    sp.dma_start(t[:, :], prm[name].rearrange("(k p) -> p k", p=C), allow_slow_non_contiguous=True).then_inc(wl, 16)
                sp.dma_start(last_node[:, :], dst.rearrange("(o g e) -> o g e", o=1, g=EI)[:, :, E // EI - 1],
                             allow_slow_non_contiguous=True).then_inc(last_in, 16)
                sp.wait_ge(wl, 16 * (5 + len(vectors)))
                sp.wait_ge(ds, 29)
                flat = lambda r: r.rearrange("(p t) -> p t", t=ET)
                sp.dma_start(flat(r_same), same_row[:, :]).then_inc(ob, 16)
                sp.dma_start(flat(r_rdst), root[:, :]).then_inc(ob, 16)
                sp.dma_start(flat(r_neg_edge), neg[:, :]).then_inc(ob, 16)
                sp.dma_start(flat(r_out), sidx[:, :]).then_inc(ob, 16)
                sp.wait_ge(cst, 8)
                sp.dma_start(node_map[0:N, :].rearrange("(p n) c -> p n c", p=P), blank[:, :, :]).then_inc(ob, 16)
                for n in (1, 2):
                    sp.dma_start(tab[n][E:E + P, :], zero_row[:, 0:n * C]).then_inc(ob, 16)
                sp.wait_ge(ob, 16 * 7)
                sp.dma_start(rows_i[:, 2, :, :], tile_rows(r_out)).then_inc(ob, 16)
                sp.wait_ge(ob, 16 * 8)

            @block.gpsimd
            def _(pool):
                pool.memset(dp_b[:, :], -1).then_inc(fill, 1)
                pool.memset(dn_b[:, :], -1).then_inc(fill, 1)
                pool.memset(ident[:, :], 0.0).then_inc(cst, 1)
                pool.memset(ones_row[:, :], 1.0).then_inc(cst, 1)
                pool.memset(zero_row[:, :], 0.0).then_inc(cst, 1)
                pool.memset(mhalf[:, :], -0.5).then_inc(cst, 1)
                pool.wait_ge(cst, 1)
                pool.affine_select(out=ident[:, :], in_=ident[:, :], compare_op=ALU.not_equal, fill=1.0,
                                   base=0, pattern=[[-1, 128]], channel_multiplier=1).then_inc(cst, 1)
                pool.iota(pos_i[:, :], pattern=[[1, ET]], base=0, channel_multiplier=ET).then_inc(cst, 1)
                pool.memset(blank[:, :, 0:1], float(E)).then_inc(cst, 1)
                pool.memset(blank[:, :, 1:2], 1.0).then_inc(cst, 1)

            @block.tensor
            def _(pe):
                pe.wait_ge(cst, 8)
                pe.wait_ge(ds, 4)
                pe.matmul(pst[0:1, 0, 0:P], pa[:, ET - 1:ET], ident[0:P, 0:P], start=True, stop=True).then_inc(ps_, 1)
                pe.matmul(pst2[0:1, 0, 0:P], sc[:, ET - 1:ET], ident[0:P, 0:P], start=True, stop=True).then_inc(ps_, 1)
                pe.wait_ge(ds, 7)
                pe.matmul(pst3[0:P, 0, 0:1], crow[0:1, 0:P], ident[0:1, 0:1], start=True, stop=True).then_inc(ps_, 1)
                for n, ready in ((0, 1), (1, 1), (2, 2)):
                    pe.wait_ge(rows_ready, ready)
                    for b in range(TB):
                        ins = pe.transpose(pst4[0:P, n, b * TR:(b + 1) * TR], rows_f[:, n, b, :], ident[0:TR, 0:TR])
                    ins.then_inc(turned, 1)

            @block.vector
            def _(dve):
                done = [0]

                def link(ins):
                    done[0] += 1
                    ins.then_inc(ds, 1)
                    dve.wait_ge(ds, done[0])

                link(dve.memset(zeros[:, :], 0.0))
                dve.wait_ge(edge_in, 16 * 7)
                link(dve.tensor_tensor(same[:, :], d_b[:, :], dp_b[:, :], ALU.is_equal))
                link(dve.tensor_tensor_scan(pa[:, :], same[:, :], zeros[:, :], 1.0, ALU.mult, ALU.add))
                link(dve.tensor_tensor_scan(sc[:, :], same[:, :], w_b[:, :], 0.0, ALU.mult, ALU.add))
                dve.memset(crow[:, :], 0.0).then_inc(ds, 1)
                done[0] += 1
                dve.wait_ge(ps_, 2)
                dve.tensor_copy(arow[:, :], pst[0:1, 0, 0:P])
                link(dve.tensor_copy(brow[:, :], pst2[0:1, 0, 0:P]))
                link(dve.tensor_tensor_scan(crow[:, 1:P + 1], arow[:, :], brow[:, :], 0.0, ALU.mult, ALU.add))
                dve.wait_ge(ps_, 3)
                link(dve.tensor_copy(carry[:, :], pst3[0:P, 0, 0:1]))
                dve.tensor_tensor_scan(dif[:, :], same[:, :], w_b[:, :], carry[:, 0:1], ALU.mult, ALU.add).then_inc(fill, 1)
                dve.wait_ge(fill, 3)
                link(dve.tensor_scalar(deg[:, :], dif[:, :], 1.0, None, ALU.add))
                link(dve.tensor_scalar(root[:, :].bitcast(I32), deg[:, :].bitcast(I32), 1, None, ALU.logical_shift_right))
                link(dve.tensor_scalar(root[:, :].bitcast(I32), root[:, :].bitcast(I32), -1, RSQRT_SEED, ALU.mult, ALU.add))
                for _ in range(3):
                    link(dve.scalar_tensor_tensor(halves[:, :], root[:, :], -0.5, deg[:, :], ALU.mult, ALU.mult))
                    link(dve.tensor_tensor(halves[:, :], halves[:, :], root[:, :], ALU.mult))
                    link(dve.scalar_tensor_tensor(root[:, :], halves[:, :], 1.5, root[:, :], ALU.add, ALU.mult))
                link(dve.tensor_copy(mval[:, :, 1], root[:, :]))
                link(dve.tensor_copy(same_row[:, :], same[:, :]))
                link(dve.tensor_tensor(last[:, :], d_b[:, :], dn_b[:, :], ALU.not_equal))
                dve.wait_ge(cst, 8)
                link(dve.tensor_copy(mval[:, :, 0], pos_i[:, :]))
                link(dve.tensor_scalar(pos_n[:, :], pos_i[:, :], float(N), None, ALU.add))
                link(dve.tensor_tensor(dif[:, :], d_b[:, :], pos_n[:, :], ALU.subtract))
                link(dve.tensor_tensor(dif[:, :], dif[:, :], last[:, :], ALU.mult))
                link(dve.tensor_tensor(sidx[:, :], dif[:, :], pos_n[:, :], ALU.add))
                link(dve.tensor_scalar(neg[:, :], last[:, :], -MASK, MASK, ALU.mult, ALU.add))
                dve.wait_ge(last_in, 16)
                link(dve.tensor_copy(last_f[:, :], last_node[:, :]))
                link(dve.tensor_scalar(count[:, :], last_f[:, :], 0.0, None, ALU.mult))
                for n in range(1, DI):
                    link(dve.scalar_tensor_tensor(count[:, :], last_f[:, :], float(n * NS * W), count[:, :], ALU.is_ge, ALU.add))
                link(dve.tensor_copy(rounds_first[:, :], count[:, :]))
                dve.wait_ge(rows_in, 32)
                dve.tensor_copy(rows_f[:, 0:2, :, :], rows_i[:, 0:2, :, :]).then_inc(rows_ready, 1)
                for n, t in enumerate((src_c, dst_c, out_c)):
                    if n == 2:
                        dve.wait_ge(ob, 16 * 8)
                        dve.tensor_copy(rows_f[:, 2, :, :], rows_i[:, 2, :, :]).then_inc(rows_ready, 1)
                    dve.wait_ge(turned, n + 1)
                    dve.tensor_copy(t[:, :], pst4[0:P, n, 0:ET])

        assert DI == EI
        x_tiles = x.rearrange("(t p g) c -> t p g c", p=P, g=G)
        masks_dense = r_neg_node.rearrange("(t g) p -> t (g p)", g=G).rearrange("(t o) w -> t o w", o=1)
        by_chunk = lambda row: row.rearrange("(k o w) -> k o w", o=1, w=CW)

        def layer_norm(ph, name, slots, groups, idx, dest, banks_at, with_stats, keep_rows=None):
            dense = idx is None
            banks = max(groups * P // CW, 1)
            gb = groups // banks
            bw = gb * P
            base = 0 if dense else stood["ln"]
            got = ph.slots(f"{name}_rows", slots) if dense else gathered["ln"]
            copied, gate = ph.slots(f"{name}_copied", slots), ph.sem(f"{name}_gate")
            mom, var, nrm, hn = (ph.slots(f"{name}_{n}", slots) for n in ("moments", "variance", "scales", "normalised"))
            tr, rl, sto, step = (ph.slots(f"{name}_{n}", slots) for n in ("transposed", "relu", "stored", "step"))
            st, rsq, kept = (ph.slots(f"{name}_{n}", slots) for n in ("stat", "rsqrt", "kept"))
            xt = ph.sb(f"{name}_x", [P, slots, groups, C])
            cols = ph.sb(f"{name}_idx", [P, slots, groups], I32)
            bs = ph.sb(f"{name}_bs", [P, slots, groups, 6])
            sm, df, q, ve, nm, rs, nb = (ph.sb(f"{name}_{n}", [P, slots, groups])
                                         for n in ("sum", "dif", "q", "ve", "nmean", "rstd", "nbias"))
            xn = ph.sb(f"{name}_xn", [P, slots, groups, C])
            ho = ph.sb(f"{name}_ho", [C, slots, groups * P])
            ps, bank0, ring = banks_at
            l_mom, l_nrm, l_turn, l_relu = (0, 2, 3, 4) if dense else (2, 3, 4, 5)
            parts = 32 if dense else 16 * groups
            rounds = DI if dense else EI
            if not dense:
                stood["ln"] += 16 * groups * EI

            def bank(j, b):
                return bank0 + (j % ring) * banks + b

            def sync(sp):
                def load(i, j):
                    wait_use(sp, hn[j], i - 1)
                    k = i * slots + j
                    sp.dma_start(xt[0:120, j, :, :], x_tiles[k, 0:120]).then_inc(got[j], 16)
                    sp.dma_start(xt[120:P, j, :, :], x_tiles[k, 120:P]).then_inc(got[j], 16)

                def store(i, j):
                    if dense:
                        to = dest[i * slots + j]
                    else:
                        to = dest[i * ES + j // 2][:, :, j % 2 * bw:(j % 2 + 1) * bw]
                    wait_use(sp, rl[j], i, banks)
                    sp.dma_start(to.rearrange("c a w -> c (a w)"), ho[:, j, :]).then_inc(sto[j], 16)

                def end():
                    for j in range(slots):
                        sp.wait_ge(sto[j], 16 * rounds)

                return slots, ([(0, load)] if dense else []) + [(l_relu + 3, store)], end

            def gpsimd(pool):
                def gather(i, j):
                    wait_use(pool, hn[j], i - 1)
                    if keep_rows is not None:
                        wait_use(pool, kept[j], i - 1, 16)
                    wait_use(pool, copied[j], i)
                    pool.sem_inc(gate, 1)
                    for g in range(groups):
                        pool.indirect_dma_start(xt[:, j, g, :], None, x[:, :],
                                                bass.IndirectOffsetOnAxis(ap=cols[:, j, g:g + 1], axis=0)).then_inc(got[j], 16)

                def scale(i, j):
                    wait_use(pool, var[j], i)
                    pool.tensor_tensor(rs[:, j, :], ve[:, j, :], mhalf[0:P, 0:groups], ALU.pow).then_inc(rsq[j], 1)

                return slots, [] if dense else [(0, gather), (l_mom, scale)], None

            def vector(dve):
                def indices(i, j):
                    dve.tensor_copy(cols[:, j, :], idx[:, bass.ds((i * slots + j) * groups, groups)]).then_inc(copied[j], 1)

                def shift(i, j):
                    wait_use(dve, rsq[j], i)
                    dve.tensor_tensor(nb[:, j, :], nm[:, j, :], rs[:, j, :], ALU.mult).then_inc(nrm[j], 1)

                def moments(i, j, between=None):
                    wait_use(dve, got[j], i, parts, base=base)
                    for g in range(groups):
                        ins = dve.bn_stats(bs[:, j, g, :], xt[:, j, g, :])
                        if g == groups - 1:
                            ins.then_inc(mom[j], 1)
                        if between:
                            between(2 * g)
                            between(2 * g + 1)

                def joined(part):
                    return [
                        lambda: [dve.tensor_tensor(sm[:, part, :], bs[:, part, :, 1], bs[:, part, :, 4], ALU.add),
                                 dve.tensor_tensor(df[:, part, :], bs[:, part, :, 1], bs[:, part, :, 4], ALU.subtract),
                                 dve.tensor_tensor(q[:, part, :], bs[:, part, :, 2], bs[:, part, :, 5], ALU.add)],
                        lambda: [dve.tensor_scalar(nm[:, part, :], sm[:, part, :], -0.5, None, ALU.mult),
                                 dve.tensor_scalar(q[:, part, :], q[:, part, :], 1.0 / C, EPS, ALU.mult, ALU.add),
                                 dve.scalar_tensor_tensor(df[:, part, :], df[:, part, :], 0.25, df[:, part, :], ALU.mult, ALU.mult)],
                        lambda: [dve.tensor_tensor(ve[:, part, :], q[:, part, :], df[:, part, :], ALU.add)]]

                def variance(i, j):
                    wait_use(dve, mom[j], i)
                    todo = joined(slice(j, j + 1))
                    for n, instructions in enumerate(todo):
                        if n:
                            wait_use(dve, step[j], i, len(todo) - 1, n)
                        instructions()[-1].then_inc(step[j] if n < len(todo) - 1 else var[j], 1)

                def pair_steps(a):
                    part = slice(a, a + 2)
                    bits = lambda t: t[:, part, :].bitcast(I32)
                    v, y, t = ve[:, part, :], rs[:, part, :], df[:, part, :]
                    todo = joined(part)
                    todo += [lambda: [dve.tensor_scalar(bits(rs), bits(ve), 1, None, ALU.logical_shift_right)],
                             lambda: [dve.tensor_scalar(bits(rs), bits(rs), -1, RSQRT_SEED, ALU.mult, ALU.add)]]
                    todo += 3 * [lambda: [dve.scalar_tensor_tensor(t, y, -0.5, v, ALU.mult, ALU.mult)],
                                 lambda: [dve.tensor_tensor(t, t, y, ALU.mult)],
                                 lambda: [dve.scalar_tensor_tensor(y, t, 1.5, y, ALU.add, ALU.mult)]]
                    todo += [lambda: [dve.tensor_tensor(nb[:, part, :], nm[:, part, :], rs[:, part, :], ALU.mult)]]
                    return todo

                def first_moments(i, j):
                    if isinstance(i, int) and i == 0 and j < 2:
                        moments(i, j)

                def scales(i, j):
                    todo = pair_steps(j) if j % 2 == 0 else []
                    last = len(todo) - 1

                    def step_(n):
                        if n > last:
                            return
                        if n == 0:
                            wait_use(dve, mom[j], i)
                            wait_use(dve, mom[j + 1], i)
                        else:
                            wait_use(dve, step[j], i, last, n)
                        todo[n]()[-1].then_inc(step[j] if n < last else nrm[j], 1)

                    i2, j2 = (i + 1 if j + 2 >= slots else i), (j + 2) % slots
                    if isinstance(i2, int) and i2 >= rounds:
                        for n in range(len(todo)):
                            step_(n)
                    else:
                        moments(i2, j2, step_)

                def column_stats(i, j):
                    for b in range(banks):
                        wait_use(dve, rl[j], i, banks, b + 1)
                        dve.sem_inc(gate, 1)
                        dve.bn_stats(stats[:, 0, (i * slots + j) * banks + b, :], ho[:, j, b * CW:(b + 1) * CW]).then_inc(st[j], 1)

                return slots, ([(0, first_moments), (2, scales)] if dense else
                               [(0, indices), (l_nrm, shift), (l_mom, moments), (l_mom, variance)]) + (
                    [(5, column_stats)] if with_stats else []), None

            def scalar(act):
                def keep_as_is(i, j):
                    wait_use(act, got[j], i, parts, base=base)
                    act.dma_start(keep_rows[i * slots + j], xt[:, j, :, :]).then_inc(kept[j], 16)

                def end():
                    for j in range(slots):
                        act.wait_ge(kept[j], 16 * rounds)

                def normalise(i, j):
                    wait_use(act, nrm[j - j % 2 if dense else j], i)
                    wait_use(act, tr[j], i - 1, banks)
                    for g in range(groups):
                        ins = act.activation(xn[:, j, g, :], xt[:, j, g, :], ACT.Identity,
                                             bias=nb[:, j, g:g + 1], scale=rs[:, j, g:g + 1])
                    ins.then_inc(hn[j], 1)

                def relu(i, j):
                    wait_use(act, sto[j], i - 1, 16)
                    if with_stats:
                        wait_use(act, st[j], i - 1, banks)
                    for b in range(banks):
                        wait_use(act, tr[j], i, banks, b + 1)
                        act.activation(ho[:, j, b * bw:(b + 1) * bw], ps[:, bank(j, b), 0:bw], ACT.Relu).then_inc(rl[j], 1)

                if keep_rows is None:
                    return slots, [(l_nrm, normalise), (l_relu, relu)], None
                return slots, [(l_nrm, keep_as_is), (l_nrm, normalise), (l_relu, relu)], end

            def tensor(pe):
                def turn(i, j):
                    wait_use(pe, hn[j], i)
                    i2, j2 = before(i, j, ring, slots)
                    wait_use(pe, rl[j2], i2, banks)
                    for b in range(banks):
                        for g in range(gb):
                            ins = pe.transpose(ps[:, bank(j, b), g * P:(g + 1) * P], xn[:, j, b * gb + g, :], ident[0:P, 0:P])
                        ins.then_inc(tr[j], 1)

                return slots, [(l_turn, turn)], None

            return dict(sync=sync, gpsimd=gpsimd, vector=vector, scalar=scalar, tensor=tensor)

        def map_scatter(ph):
            cp, gate, sem = ph.slots("ms_copied", QS), ph.sem("ms_gate"), gathered["map_out"]
            cols, vals = ph.sb("ms_idx", [P, QS, QG], I32), ph.sb("ms_val", [P, QS, QG, 2])

            def gpsimd(pool):
                def scatter(i, j):
                    wait_use(pool, cp[j], i, 2)
                    pool.sem_inc(gate, 1)
                    for m in range(QG):
                        pool.indirect_dma_start(node_map[:, :], bass.IndirectOffsetOnAxis(ap=cols[:, j, m:m + 1], axis=0),
                                                vals[:, j, m, :], None).then_inc(sem[j], 16)

                def end():
                    for j in range(QS):
                        pool.wait_ge(sem[j], 16 * QG * EI)

                return QS, [(0, scatter)], end

            def vector(dve):
                def entries(i, j):
                    wait_use(dve, sem[j], i - 1, 16 * QG)
                    dve.sem_inc(gate, 1)
                    at = bass.ds((i * QS + j) * QG, QG)
                    dve.tensor_copy(cols[:, j, :], sidx[:, at]).then_inc(cp[j], 1)
                    dve.tensor_copy(vals[:, j, :, :], mval[:, at, :]).then_inc(cp[j], 1)

                return QS, [(0, entries)], None

            return dict(gpsimd=gpsimd, vector=vector)

        def map_gather(ph):
            cp, gate, got = ph.slots("mg_copied", QS), ph.sem("mg_gate"), ph.slots("mg_taken", QS)
            gate_t = ph.sem("mg_gate_take")
            sem = gathered["map_in"]
            cols, vals = ph.sb("mg_idx", [P, QS, QG], I32), ph.sb("mg_val", [P, QS, QG, 2])

            def gpsimd(pool):
                def gather(i, j):
                    wait_use(pool, got[j], i - 1)
                    wait_use(pool, cp[j], i)
                    pool.sem_inc(gate, 1)
                    for m in range(QG):
                        pool.indirect_dma_start(vals[:, j, m, :], None, node_map[0:N, :],
                                                bass.IndirectOffsetOnAxis(ap=cols[:, j, m:m + 1], axis=0)).then_inc(sem[j], 16)

                return QS, [(0, gather)], None

            def vector(dve):
                def indices(i, j):
                    dve.tensor_copy(cols[:, j, :], s_b[:, bass.ds((i * QS + j) * QG, QG)]).then_inc(cp[j], 1)

                def take(i, j):
                    wait_use(dve, sem[j], i, 16 * QG)
                    dve.sem_inc(gate_t, 1)
                    dve.tensor_copy(msrc[:, bass.ds((i * QS + j) * QG, QG), :], vals[:, j, :, :]).then_inc(got[j], 1)

                return QS, [(0, indices), (2, take)], None

            return dict(gpsimd=gpsimd, vector=vector)

        def dense_layer(ph, n, kb, mb, h_in, h_out, ps):
            wf, bf = wfold[n], bfold[n]
            per = mb * CH
            late = 0 if n == 1 else 2 * NS
            got, mm, rl = ph.slots("dn_in", NS), ph.slots("dn_product", NS), ph.slots("dn_relu", NS)
            st, sto, gate = ph.slots("dn_stat", NS), ph.slots("dn_stored", NS), ph.sem("dn_gate")
            spl = ph.slots("dn_split", NS)
            split = n == 2
            ahead = late + split
            hi = ph.sb("dn_hi", [C, NS, kb, W])
            if split:
                top, rest = (ph.sb(f"dn_{x}", [C, 2, kb, W], FR) for x in ("top", "rest"))
                cut = ph.sb("dn_cut", [C, CW], I32)
            ho = ph.sb("dn_ho", [C, NS, mb, W])
            mk = ph.sb("dn_mask", [1, NS, W], BF)

            def sync(sp):
                def load(i, j):
                    wait_use(sp, mm[j], i - 1, per)
                    k = i * NS + j
                    sp.dma_start(hi[:, j, :, :], h_in[k]).then_inc(got[j], 16)
                    sp.dma_start(mk[:, j, :], masks_dense[k]).then_inc(got[j], 16)

                def store(i, j):
                    wait_use(sp, rl[j], i, per)
                    sp.dma_start(h_out[i * NS + j], ho[:, j, :, :]).then_inc(sto[j], 16)

                def end():
                    for j in range(NS):
                        sp.wait_ge(sto[j], 16 * DI)

                return NS, [(late, load), (ahead + 3, store)], end

            def tensor(pe):
                def products(i, j):
                    wait_use(pe, got[j], i, 32)
                    if split:
                        wait_use(pe, spl[j], i, 3 * kb * CH)
                    for u in range(per):
                        m, c = divmod(u, CH)
                        if u >= 2:
                            wait_use(pe, rl[j], i, per, u - 1)
                        else:
                            i1, j1 = before(i, j, 1, NS)
                            wait_use(pe, rl[j1], i1, per, per - 1 + u)
                        o = ps[:, u % 2, 0:CW]
                        pe.matmul(o, ones_row[:, :], mk[:, j, c * CW:(c + 1) * CW], start=True, stop=False)
                        mc, cc = slice(m * C, (m + 1) * C), slice(c * CW, (c + 1) * CW)
                        terms = [(wf[:, k, mc], hi[:, j, k, cc]) for k in range(kb)]
                        if split:
                            w_top, w_rest = wparts
                            terms = [(a[:, k, mc], b[:, k, cc]) for k in range(kb) for a, b in
                                     ((w_top, top[:, j % 2]), (w_top, rest[:, j % 2]), (w_rest, top[:, j % 2]))]
                        for t, (a, b) in enumerate(terms):
                            ins = pe.matmul(o, a, b, start=False, stop=t == len(terms) - 1)
                        ins.then_inc(mm[j], 1)

                return NS, [(ahead, products)], None

            def scalar(act):
                def relu(i, j):
                    wait_use(act, sto[j], i - 1, 16)
                    wait_use(act, st[j], i - 1, per)
                    for u in range(per):
                        m, c = divmod(u, CH)
                        wait_use(act, mm[j], i, per, u + 1)
                        act.activation(ho[:, j, m, c * CW:(c + 1) * CW], ps[:, u % 2, 0:CW],
                                       ACT.Relu, bias=bf[:, m:m + 1]).then_inc(rl[j], 1)

                return NS, [(ahead, relu)], None

            def vector(dve):
                def statistics(i, j):
                    for u in range(per):
                        m, c = divmod(u, CH)
                        wait_use(dve, rl[j], i, per, u + 1)
                        dve.sem_inc(gate, 1)
                        dve.bn_stats(stats[:, m, (i * NS + j) * CH + c, :], ho[:, j, m, c * CW:(c + 1) * CW]).then_inc(st[j], 1)

                return NS, [(ahead + 1, statistics)], None

            def vector_split(dve):
                def parts(i, j):
                    wait_use(dve, got[j], i, 32)
                    i2, j2 = before(i, j, 2, NS)
                    wait_use(dve, mm[j2], i2, per)
                    for u in range(kb * CH):
                        k, c = divmod(u, CH)
                        cc = slice(c * CW, (c + 1) * CW)
                        x_u, top_u = hi[:, j, k, cc], top[:, j % 2, k, cc]
                        dve.tensor_scalar(cut[:, :], x_u.bitcast(I32), TOP_BITS, None, ALU.bitwise_and).then_inc(spl[j], 1)
                        wait_use(dve, spl[j], i, 3 * kb * CH, 3 * u + 1)
                        dve.tensor_copy(top_u, cut[:, :].bitcast(FP)).then_inc(spl[j], 1)
                        wait_use(dve, spl[j], i, 3 * kb * CH, 3 * u + 2)
                        dve.tensor_tensor(rest[:, j % 2, k, cc], x_u, top_u.bitcast(FP), ALU.subtract).then_inc(spl[j], 1)

                return NS, [(late, parts)], None

            work = dict(sync=sync, tensor=tensor, scalar=scalar, vector=vector)
            return (dict(vector=vector_split), work) if split else work

        def edge_layer(ph, n, ps, slots):
            kb, mb = (1, 2, 2)[n - 1], (2, 2, 1)[n - 1]
            rounds = EC // slots
            ks = n - 1
            l_turn, l_src, l_sum, l_rel, l_dst, l_out = {1: (0, 0, 1, 1, 2, 3), 2: (1, 2, 3, 4, 5, 6), 3: (1, 1, 2, 2, 3, 4)}[n]
            r_coef = r_msg if n == 1 else ew
            base = stood["src"]
            in_a, in_b, in_c = ph.slots("ed_in_a", slots), ph.slots("ed_in_b", slots), ph.slots("ed_in_c", slots)
            copied, gate, gate_d = ph.slots("ed_copied", slots), ph.sem("ed_gate"), ph.sem("ed_gate_d")
            gate_l = ph.sem("ed_gate_load")
            gat = gathered["src"]
            sems = "turned z_affine z src_product src_relu src_stored affine msg scan rel rel_out dst_affine dst_z"
            tu, za, zz, mm_s, rl_s, sto_s, aff, msg, scn, mm_r, ev_r, da, dz = (ph.slots(f"ed_{x}", slots) for x in sems.split())
            mm_d, rl_d, st_d, sto_d, tr, ev_t, sto_t = (ph.slots(f"ed_{x}", slots) for x in
                                                        "dst_product dst_relu dst_stat dst_stored rows rows_out rows_stored".split())
            ss = ph.sb("ed_same", [C, slots, CW], BF)
            cf = ph.sb("ed_coef", [C, slots, CW])
            xa = ph.sb("ed_xa", [C, slots, kb, CW])
            se = ph.sb("ed_sum", [C, slots, kb, CW])
            hd_in = ph.sb("ed_hd", [C, slots, kb, CW])
            mk = ph.sb("ed_mask", [1, slots, CW], BF)
            ho_d = ph.sb("ed_ho", [C, slots, mb, CW])
            hsi = ph.sb("ed_hs", [C, slots, max(ks, 1), CW])
            zero = ph.sb("ed_zero", [C, 1])
            z0 = ph.sem("ed_zero_set")
            if n == 1:
                rd = ph.sb("ed_rd", [C, slots, CW])
                ag = ph.sb("ed_agg", [C, slots, 1, CW])
            else:
                tg = ph.sb("ed_gathered", [P, slots, EG, ks * C])
                cols = ph.sb("ed_idx", [P, slots, EG], I32)
                ho_s = ph.sb("ed_ho_src", [C, slots, 2, CW])
                stood["src"] += 16 * EG * rounds
            if n == 2:
                inv = ph.sb("ed_inv", [C, slots, CW])
                ag = ph.sb("ed_rel", [C, slots, 2, CW])
            if n < 3:
                tb = ph.sb("ed_rows", [P, slots, EG, kb * C])
                tiles = tab[n][0:E, :].rearrange("(t g p) c -> t p g c", p=P, g=EG)
                halves = kb
                hg = EG // halves
            BS, BD, BT, BG = 3, 5, 7, 2
            n_b = 48 if n == 1 else 32
            n_c = 32
            h_src = (hsi, in_a, 16 + 16 * (n == 2)) if n == 1 else (ho_s, rl_s, 2)

            def line(row, k):
                return by_chunk(row)[k].broadcast_to([C, CW])

            def sync(sp):
                def load_source(i, j):
                    k = i * slots + j
                    wait_use(sp, aff[j] if n == 1 else mm_s[j], i - 1, kb if n == 1 else 2)
                    sp.dma_start(hsi[:, j, :, :], hs[max(n - 2, 0)][k]).then_inc(in_a[j], 16)
                    if n == 2:
                        sp.dma_start(inv[:, j, :], line(r_isrc, k)).then_inc(in_a[j], 16)

                def load_rows(i, j):
                    k = i * slots + j
                    if n == 1:
                        wait_use(sp, dz[j], i - 1, 4)
                    else:
                        wait_use(sp, scn[j], i - 1, kb)
                    sp.sem_inc(gate_l, 1)
                    sp.dma_start(ss[:, j, :], line(r_same, k)).then_inc(in_b[j], 16)
                    sp.dma_start(cf[:, j, :], line(r_coef, k)).then_inc(in_b[j], 16)
                    if n == 1:
                        sp.dma_start(rd[:, j, :], line(r_rdst, k)).then_inc(in_b[j], 16)

                def load_dst(i, j):
                    k = i * slots + j
                    wait_use(sp, mm_d[j], i - 1, mb)
                    sp.dma_start(hd_in[:, j, :, :], hd[n - 1][k]).then_inc(in_c[j], 16)
                    sp.dma_start(mk[:, j, :], by_chunk(r_neg_edge)[k]).then_inc(in_c[j], 16)

                return slots, [(max(l_src, l_sum) if n == 1 else l_src, load_source), (l_sum, load_rows), (l_dst, load_dst)], None

            def gpsimd(pool):
                if n == 1:
                    return slots, [], None

                def gather(i, j):
                    wait_use(pool, tu[j], i - 1, ks)
                    pool.sem_inc(gate, 1)
                    pool.tensor_copy(cols[:, j, :], pos_c[:, bass.ds((i * slots + j) * EG, EG)]).then_inc(copied[j], 1)
                    wait_use(pool, copied[j], i)
                    pool.sem_inc(gate, 1)
                    for g in range(EG):
                        pool.indirect_dma_start(tg[:, j, g, :], None, tab[n - 1][:, :],
                                                bass.IndirectOffsetOnAxis(ap=cols[:, j, g:g + 1], axis=0)).then_inc(gat[j], 16)

                return slots, [(0, gather)], None

            def tensor(pe):
                def turn(i, j):
                    wait_use(pe, gat[j], i, 16 * EG, base=base)
                    i1, j1 = before(i, j, 1, slots)
                    wait_use(pe, zz[j1], i1, 2)
                    for g in range(EG):
                        ins = pe.transpose(ps[:, BG, g * P:(g + 1) * P], tg[:, j, g, :], ident[0:P, 0:P])
                    ins.then_inc(tu[j], 1)

                def source(i, j):
                    i1, j1 = before(i, j, 1, slots)
                    if n == 2:
                        wait_use(pe, zz[j], i, 2)
                    else:
                        wait_use(pe, in_a[j], i, 16)
                        wait_use(pe, gat[j], i, 16 * EG, base=base)
                    for m in range(2):
                        wait_use(pe, rl_s[j1], i1, 2, m + 1)
                        o = ps[:, BS + m, 0:CW]
                        if n == 3:
                            for g in range(EG):
                                ins = pe.matmul(ps[:, BS + m, g * P:(g + 1) * P], tg[:, j, g, m * C:(m + 1) * C], ident[0:P, 0:P],
                                                start=g == 0, stop=False, is_transpose=True, skip_group_check=True)
                            ins.then_inc(tu[j], 1)
                        for k in range(ks):
                            w = w1 if n == 2 else wfold[2]
                            ins = pe.matmul(o, w[:, k, m * C:(m + 1) * C], hsi[:, j, k, :],
                                            start=n == 2 and k == 0, stop=k == ks - 1, skip_group_check=n == 3)
                        ins.then_inc(mm_s[j], 1)

                def rel(i, j):
                    i1, j1 = before(i, j, 1, slots)
                    for m in range(mb):
                        wait_use(pe, rl_d[j1], i1, mb, m + 1)
                        for k in range(kb):
                            wait_use(pe, scn[j], i, kb, k + 1)
                            ins = pe.matmul(ps[:, BD + m, 0:CW], wrel[n][:, k, m * C:(m + 1) * C], se[:, j, k, :],
                                            start=k == 0, stop=k == kb - 1)
                        ins.then_inc(mm_r[j], 1)

                def dst(i, j):
                    i1, j1 = before(i, j, 1, slots)
                    wait_use(pe, in_c[j], i, n_c)
                    if n == 1:
                        wait_use(pe, dz[j], i, 4)
                    if n == 3:
                        wait_use(pe, scn[j], i, kb)
                    for m in range(mb):
                        mc = slice(m * C, (m + 1) * C)
                        if n == 2:
                            wait_use(pe, ev_r[j], i, 2, m + 1)
                        else:
                            wait_use(pe, rl_d[j1], i1, mb, m + 1)
                        o = ps[:, BD + m, 0:CW]
                        pe.matmul(o, ones_row[:, :], mk[:, j, :], start=n != 2, stop=False, skip_group_check=n == 2)
                        terms = [((w1 if n == 1 else wfold[n])[:, k, mc], hd_in[:, j, k, :]) for k in range(kb)]
                        if n == 3:
                            terms += [(wrel[n][:, k, mc], se[:, j, k, :]) for k in range(kb)]
                        for t, (a, b) in enumerate(terms):
                            ins = pe.matmul(o, a, b, start=False, stop=t == len(terms) - 1, skip_group_check=n == 2)
                        ins.then_inc(mm_d[j], 1)

                def table(half):
                    def turn_rows(i, j):
                        if half == 0:
                            i1, j1 = before(i, j, 1, slots)
                            wait_use(pe, ev_t[j1], i1, halves)
                            if n == 1:
                                wait_use(pe, dz[j], i, 4, 1)
                            else:
                                wait_use(pe, ev_r[j], i, 2)
                        else:
                            wait_use(pe, ev_t[j], i, halves, half)
                        for g in range(hg):
                            for k in range(kb):
                                e = (half * hg + g) * P
                                ins = pe.transpose(ps[0:P, BT, (g * kb + k) * C:(g * kb + k + 1) * C], ag[:, j, k, e:e + P], ident[:, :])
                        ins.then_inc(tr[j], 1)

                    return turn_rows

                stages = [(l_dst, table(0))] if n < 3 else []
                stages += [(l_dst, dst)]
                stages += [(l_dst, table(1))] if n == 2 else []
                stages += [(l_turn, turn)] if n == 2 else []
                stages += [(l_src, source)] if n > 1 else []
                stages += [(l_rel, rel)] if n == 2 else []
                return slots, stages, None

            def vector(dve):
                dve.memset(zero[:, :], 0.0).then_inc(z0, 1)
                dve.wait_ge(z0, 1)

                def source_z(i, j):
                    wait_use(dve, in_a[j], i, 32)
                    wait_use(dve, za[j], i)
                    dve.tensor_tensor(hsi[:, j, 0, :], hsi[:, j, 0, :], inv[:, j, :], ALU.mult).then_inc(zz[j], 1)
                    wait_use(dve, zz[j], i, 2, 1)
                    wait_use(dve, tu[j], i)
                    dve.tensor_tensor(hsi[:, j, 0, :], hsi[:, j, 0, :], ps[:, BG, 0:CW], ALU.add).then_inc(zz[j], 1)

                def sums(i, j):
                    wait_use(dve, in_b[j], i, n_b)
                    for k in range(kb):
                        wait_use(dve, aff[j], i, kb, k + 1)
                        dve.tensor_tensor(xa[:, j, k, :], xa[:, j, k, :], cf[:, j, :], ALU.mult).then_inc(msg[j], 1)
                    if n == 1:
                        wait_use(dve, dz[j], i - 1, 4)
                    elif n == 2:
                        wait_use(dve, mm_r[j], i - 1, mb)
                    else:
                        wait_use(dve, mm_d[j], i - 1, mb)
                    i1, j1 = before(i, j, 1, slots)
                    wait_use(dve, scn[j1], i1, kb)
                    for k in range(kb):
                        wait_use(dve, msg[j], i, kb, k + 1)
                        fresh = isinstance(i1, int) and i1 < 0
                        start = zero[:, 0:1] if fresh else se[:, j1, k, CW - 1:CW]
                        dve.tensor_tensor_scan(se[:, j, k, :], ss[:, j, :], xa[:, j, k, :], start, ALU.mult, ALU.add).then_inc(scn[j], 1)
                    if n == 1:
                        wait_use(dve, scn[j], i)
                        wait_use(dve, tr[j], i - 1)
                        dve.tensor_tensor(ag[:, j, 0, :], se[:, j, 0, :], rd[:, j, :], ALU.mult).then_inc(dz[j], 1)
                        wait_use(dve, da[j], i)
                        dve.tensor_tensor(hd_in[:, j, 0, :], hd_in[:, j, 0, :], rd[:, j, :], ALU.mult).then_inc(dz[j], 1)
                        wait_use(dve, dz[j], i, 4, 2)
                        dve.tensor_tensor(hd_in[:, j, 0, :], hd_in[:, j, 0, :], se[:, j, 0, :], ALU.add).then_inc(dz[j], 1)
                        wait_use(dve, dz[j], i, 4, 3)
                        dve.tensor_tensor(hd_in[:, j, 0, :], hd_in[:, j, 0, :], rd[:, j, :], ALU.mult).then_inc(dz[j], 1)

                def statistics(i, j):
                    for m in range(mb):
                        wait_use(dve, rl_d[j], i, mb, m + 1)
                        dve.sem_inc(gate_d, 1)
                        dve.bn_stats(stats[:, m, NT * CH + i * slots + j, :], ho_d[:, j, m, :]).then_inc(st_d[j], 1)

                stages = [(l_dst, statistics)]
                stages += [(l_turn, source_z)] if n == 2 else []
                stages += [(l_sum, sums)]
                return slots, stages[::-1] if n == 1 else stages, None

            def scalar(act):
                def store_source(i, j):
                    wait_use(act, rl_s[j], i, 2)
                    act.dma_start(hs[1][i * slots + j], ho_s[:, j, :, :]).then_inc(sto_s[j], 16)

                def store_dst(i, j):
                    wait_use(act, rl_d[j], i, mb)
                    act.dma_start(hd[n][i * slots + j], ho_d[:, j, :, :]).then_inc(sto_d[j], 16)

                def store_table(i, j):
                    wait_use(act, ev_t[j], i, halves)
                    act.dma_start(tiles[i * slots + j], tb[:, j, :, :]).then_inc(sto_t[j], 16)

                def end():
                    for j in range(slots):
                        act.wait_ge(sto_d[j], 16 * rounds)
                        if n < 3:
                            act.wait_ge(sto_t[j], 16 * rounds)
                        if n == 2:
                            act.wait_ge(sto_s[j], 16 * rounds)

                def source_affine(i, j):
                    wait_use(act, in_a[j], i, 32)
                    act.activation(hsi[:, j, 0, :], hsi[:, j, 0, :], ACT.Identity, bias=sft[0][:, 0:1], scale=sca[0][:, 0:1]).then_inc(za[j], 1)

                def source_relu(i, j):
                    wait_use(act, aff[j], i - 1, kb)
                    if n == 2:
                        wait_use(act, sto_s[j], i - 1, 16)
                    for m in range(2):
                        wait_use(act, mm_s[j], i, 2, m + 1)
                        b = bias[1] if n == 2 else bfold[2]
                        act.activation(ho_s[:, j, m, :], ps[:, BS + m, 0:CW], ACT.Relu, bias=b[:, m:m + 1]).then_inc(rl_s[j], 1)

                def affine(i, j):
                    src_t, src_sem, src_n = h_src
                    wait_use(act, scn[j], i - 1, kb)
                    for k in range(kb):
                        wait_use(act, src_sem[j], i, src_n, src_n if n == 1 else k + 1)
                        act.activation(xa[:, j, k, :], src_t[:, j, k, :], ACT.Identity, bias=sft[n - 1][:, k:k + 1],
                                       scale=sca[n - 1][:, k:k + 1]).then_inc(aff[j], 1)
                    if n == 1:
                        wait_use(act, in_c[j], i, n_c)
                        act.activation(hd_in[:, j, 0, :], hd_in[:, j, 0, :], ACT.Identity, bias=sft[0][:, 0:1],
                                       scale=sca[0][:, 0:1]).then_inc(da[j], 1)

                def rel_out(i, j):
                    wait_use(act, tr[j], i - 1, halves)
                    for m in range(2):
                        wait_use(act, mm_r[j], i, 2, m + 1)
                        act.activation(ag[:, j, m, :], ps[:, BD + m, 0:CW], ACT.Copy).then_inc(ev_r[j], 1)

                def table_out(half):
                    def rows_out(i, j):
                        if half == 0:
                            wait_use(act, sto_t[j], i - 1, 16)
                        wait_use(act, tr[j], i, halves, half + 1)
                        act.activation(tb[:, j, half * hg:(half + 1) * hg, :],
                                       ps[0:P, BT, 0:hg * kb * C].rearrange("p (g c) -> p g c", g=hg), ACT.Copy).then_inc(ev_t[j], 1)

                    return rows_out

                def dst_relu(i, j):
                    wait_use(act, sto_d[j], i - 1, 16)
                    wait_use(act, st_d[j], i - 1, mb)
                    b = bias[1] if n == 1 else bfold[n]
                    for m in range(mb):
                        wait_use(act, mm_d[j], i, mb, m + 1)
                        act.activation(ho_d[:, j, m, :], ps[:, BD + m, 0:CW], ACT.Relu, bias=b[:, m:m + 1]).then_inc(rl_d[j], 1)

                stages = [(l_dst, table_out(0))] if n < 3 else []
                stages += [(l_dst, dst_relu)]
                stages += [(l_dst, table_out(1))] if n == 2 else []
                stages += [(l_turn, source_affine)] if n == 2 else []
                stages += [(l_src, source_relu)] if n > 1 else []
                stages += [(l_src if n > 1 else l_sum, affine)]
                stages += [(l_rel, rel_out)] if n == 2 else []
                stages += [(l_src + 1, store_source)] if n == 2 else []
                stages += [(l_out, store_table)] if n < 3 else []
                if n == 1:
                    stages = stages[-2:-1] + stages[:-2] + stages[-1:]
                return slots, stages + [(l_out, store_dst)], end

            return dict(sync=sync, gpsimd=gpsimd, tensor=tensor, vector=vector, scalar=scalar)

        def fold(n, blocks, groups, weight, folded, b_in, b_out, masks=False):
            ratio = groups * CW / N
            with Phase(nc, f"fold{n}") as ph:
                s, pwd, pd = ph.sem("steps"), ph.sem("pow"), ph.sem("bias")
                mv = ph.sb("mv", [C, blocks, 2])
                t1, t2, t3 = (ph.sb(f"t{k}", [C, blocks]) for k in (1, 2, 3))
                ps = ph.pb("ps", 2)
                cut = ph.sb("cut", [C, 2, H1], I32)
                if masks:
                    node_in, nd, npe = ph.sem("node_in"), ph.sem("node_dve"), ph.sem("node_pe")
                    node_out = ph.slots("node_out", 2)
                    flags = ph.sb("flags", [P, NT * G])
                    nmap = ph.sb("nmap", [P, NT, 2 * G])
                    nrow = ph.sb("neg_rows", [128, 2, P], BF)
                    pm = ph.pb("pm", 2)
                    blocks_m = [(128 * b, min(128, NT * G - 128 * b)) for b in range(-(-(NT * G) // 128))]
                block = ph.start()

                @block.sync
                def _(sp):
                    if not masks:
                        return
                    sp.dma_start(nmap[:, :, :], node_map[0:N, :].rearrange("(t p g) c -> p t (g c)", p=P, g=G)).then_inc(node_in, 16)
                    for b, (at, width) in enumerate(blocks_m):
                        sp.wait_ge(nd, b + 2)
                        sp.dma_start(r_neg_node[at:at + width, :], nrow[0:width, b % 2, :]).then_inc(node_out[b % 2], 16)
                    for j in range(min(2, len(blocks_m))):
                        sp.wait_ge(node_out[j], 16 * ((len(blocks_m) - j + 1) // 2))

                @block.vector
                def _(dve):
                    done = [0]

                    def link(ins):
                        done[0] += 1
                        ins.then_inc(s, 1)
                        dve.wait_ge(s, done[0])

                    if masks:
                        dve.wait_ge(node_in, 16)
                        dve.tensor_scalar(flags[:, :].rearrange("p (t g) -> p t g", g=G),
                                          nmap[:, :, :].rearrange("p t (g c) -> p t g c", c=2)[:, :, :, 0],
                                          float(E), None, ALU.is_lt).then_inc(nd, 1)
                        for b, (at, width) in enumerate(blocks_m):
                            dve.wait_ge(npe, b + 1)
                            if b >= 2:
                                dve.wait_ge(node_out[b % 2], 16 * (b // 2))
                            dve.tensor_scalar(nrow[0:width, b % 2, :], pm[0:width, b % 2, 0:P], MASK, None, ALU.mult).then_inc(nd, 1)
                    for b in range(blocks):
                        link(dve.bn_aggr(mv[:, b, :], stats[:, b, 0:groups, :].rearrange("p g s -> p (g s)")))
                    mean, var = mv[:, :, 0], mv[:, :, 1]
                    link(dve.tensor_tensor(t1[:, :], mean, mean, ALU.mult))
                    link(dve.tensor_tensor(t2[:, :], var, t1[:, :], ALU.add))
                    link(dve.tensor_scalar(t2[:, :], t2[:, :], ratio, None, ALU.mult))
                    link(dve.tensor_scalar(t1[:, :], mean, ratio, None, ALU.mult))
                    link(dve.tensor_tensor(t3[:, :], t1[:, :], t1[:, :], ALU.mult))
                    link(dve.tensor_tensor(t2[:, :], t2[:, :], t3[:, :], ALU.subtract))
                    link(dve.tensor_scalar(t2[:, :], t2[:, :], 0.0, EPS, ALU.max, ALU.add))
                    dve.wait_ge(pwd, 1)
                    link(dve.tensor_tensor(sca[n][:, :], gam[n][:, :], t3[:, :], ALU.mult))
                    link(dve.tensor_tensor(t1[:, :], t1[:, :], sca[n][:, :], ALU.mult))
                    link(dve.tensor_tensor(sft[n][:, :], bet[n][:, :], t1[:, :], ALU.subtract))
                    if weight is None:
                        return
                    for k in range(blocks):
                        link(dve.tensor_scalar(folded[:, k, :], weight[:, k, :], sca[n][:, k:k + 1], None, ALU.mult))
                    if n == 1:
                        w_top, w_rest = wparts
                        link(dve.tensor_scalar(cut[:, :, :], folded[:, :, :].bitcast(I32), TOP_BITS, None, ALU.bitwise_and))
                        link(dve.tensor_copy(w_top[:, :, :], cut[:, :, :].bitcast(FP)))
                        link(dve.tensor_tensor(w_rest[:, :, :], folded[:, :, :], w_top[:, :, :].bitcast(FP), ALU.subtract))
                    for m in range(b_in.shape[1]):
                        dve.wait_ge(pd, m + 1)
                        link(dve.tensor_tensor(b_out[:, m:m + 1], b_in[:, m:m + 1], ps[:, m, 0:1], ALU.add))

                @block.gpsimd
                def _(pool):
                    pool.wait_ge(s, blocks + 7)
                    pool.tensor_tensor(t3[:, :], t2[:, :], mhalf[:, 0:blocks], ALU.pow).then_inc(pwd, 1)

                @block.tensor
                def _(pe):
                    if masks:
                        pe.wait_ge(nd, 1)
                        for b, (at, width) in enumerate(blocks_m):
                            if b >= 2:
                                pe.wait_ge(nd, b)
                            pe.matmul(pm[0:width, b % 2, 0:P], flags[:, at:at + width], ident[0:P, 0:P],
                                      start=True, stop=True).then_inc(npe, 1)
                    if weight is None:
                        return
                    pe.wait_ge(s, blocks + 10)
                    for m in range(b_in.shape[1]):
                        for k in range(blocks):
                            ins = pe.matmul(ps[:, m, 0:1], weight[:, k, m * C:(m + 1) * C], sft[n][:, k:k + 1],
                                            start=k == 0, stop=k == blocks - 1)
                        ins.then_inc(pd, 1)

        def source_rows():
            with Phase(nc, "sources") as ph:
                rows, pos_io, steps = ph.sem("rows"), ph.sem("positions_io"), ph.sem("steps")
                isrc, cmsg = ph.sb("isrc", [P, ET]), ph.sb("cmsg", [P, ET])
                posi = ph.sb("posi", [P, ET], I32)
                rows_i, rows_f = ph.sb("rows_i", [TR, TB, P], I32), ph.sb("rows_f", [TR, TB, P])
                pt, turned = ph.pb("pt", 1), ph.sem("turned")
                block = ph.start()

                @block.vector
                def _(dve):
                    dve.tensor_copy(posi[:, :], msrc[:, :, 0]).then_inc(steps, 1)
                    dve.tensor_tensor(isrc[:, :], msrc[:, :, 1], msrc[:, :, 1], ALU.mult).then_inc(steps, 1)
                    dve.tensor_tensor(cmsg[:, :], w_b[:, :], msrc[:, :, 1], ALU.mult).then_inc(steps, 1)
                    dve.wait_ge(pos_io, 32)
                    dve.tensor_copy(rows_f[:, :, :], rows_i[:, :, :]).then_inc(steps, 1)
                    dve.wait_ge(turned, 1)
                    dve.tensor_copy(pos_c[:, :], pt[0:P, 0, 0:ET]).then_inc(steps, 1)

                @block.scalar
                def _(act):
                    flat = lambda r: r.rearrange("(p t) -> p t", t=ET)
                    act.wait_ge(steps, 3)
                    act.dma_start(flat(r_msg), cmsg[:, :]).then_inc(rows, 16)
                    act.dma_start(flat(r_isrc), isrc[:, :]).then_inc(rows, 16)
                    act.wait_ge(rows, 32)

                @block.sync
                def _(sp):
                    sp.wait_ge(steps, 1)
                    sp.dma_start(r_pos.rearrange("(p t) -> p t", t=ET), posi[:, :]).then_inc(pos_io, 16)
                    sp.wait_ge(pos_io, 16)
                    sp.dma_start(rows_i[:, :, :], tile_rows(r_pos)).then_inc(pos_io, 16)
                    sp.wait_ge(pos_io, 32)

                @block.tensor
                def _(pe):
                    pe.wait_ge(steps, 4)
                    for b in range(TB):
                        ins = pe.transpose(pt[0:P, 0, b * TR:(b + 1) * TR], rows_f[:, b, :], ident[0:TR, 0:TR])
                    ins.then_inc(turned, 1)

        def output(ph, name, slots, groups, bank0, ps):
            dense = name == "od"
            banks = max(groups // EG, 1)
            gb = groups // banks
            rounds = DI if dense else EI
            h_in = h3 if dense else hd[3]
            got, gx = ph.slots(f"{name}_in", slots), ph.slots(f"{name}_x", slots)
            aff, tr, sm = (ph.slots(f"{name}_{n}", slots) for n in ("affine", "turned", "summed"))
            sto, gate = dense_stored, ph.sem(f"{name}_gate")
            hi = ph.sb(f"{name}_hi", [C, slots, groups * P])
            xt = ph.sb(f"{name}_xt", [P, slots, groups, C])
            ot = ph.sb(f"{name}_ot", [P, slots, groups, C]) if dense else None
            out_rows = out[0:N, :].rearrange("(t p g) c -> t p g c", p=P, g=G)

            def sync(sp):
                def load(i, j):
                    k = i * slots + j
                    wait_use(sp, tr[j], i - 1, banks)
                    h = h_in[k] if dense else h_in[i * ES + j // 2][:, :, j % 2 * QG * P:(j % 2 + 1) * QG * P]
                    sp.dma_start(hi[:, j, :], h.rearrange("c a w -> c (a w)")).then_inc(got[j], 16)
                    wait_use(sp, sm[j], i - 1, banks)
                    if dense:
                        sp.dma_start(xt[0:120, j, :, :], x_tiles[k, 0:120]).then_inc(gx[j], 16)
                        sp.dma_start(xt[120:P, j, :, :], x_tiles[k, 120:P]).then_inc(gx[j], 16)
                    else:
                        sp.dma_start(xt[:, j, :, :], x_dst[k]).then_inc(gx[j], 16)

                def store(i, j):
                    k = i * slots + j
                    wait_use(sp, sm[j], i, banks)
                    sp.dma_start(out_rows[k, 0:120], ot[0:120, j, :, :]).then_inc(sto[j], 16)
                    sp.dma_start(out_rows[k, 120:P], ot[120:P, j, :, :]).then_inc(sto[j], 16)

                def end():
                    for j in range(slots):
                        sp.wait_ge(sto[j], 32 * rounds)

                return slots, [(0, load)] + ([(slots - 1, store)] if dense else []), end if dense else None

            def gpsimd(pool):
                def end():
                    per = ET // rounds
                    for g in range(rounds):
                        for j in range(slots):
                            pool.wait_ge(sm[j], g + 1)
                        first = pool.value_load(rounds_first[0:1, g:g + 1], min_val=0, max_val=DI - 1)
                        for s in dense_stored:
                            pool.wait_ge(s, first * 32 + 32)
                        pool.sem_inc(gate, 1)
                        for t in range(g * per, (g + 1) * per):
                            pool.indirect_dma_start(out[:, :], bass.IndirectOffsetOnAxis(ap=out_c[:, t:t + 1], axis=0),
                                                    rows_dst[:, t, :], None).then_inc(gathered["out"][0], 16)
                    pool.wait_ge(gathered["out"][0], 16 * ET)

                return slots, [], None if dense else end

            def scalar(act):
                def affine(i, j):
                    wait_use(act, got[j], i, 16)
                    act.activation(hi[:, j, :], hi[:, j, :], ACT.Identity, bias=sft[3][:, 0:1], scale=sca[3][:, 0:1]).then_inc(aff[j], 1)

                return slots, [(0, affine)], None

            def tensor(pe):
                def turn(i, j):
                    wait_use(pe, aff[j], i)
                    i2, j2 = before(i, j, 2, slots)
                    wait_use(pe, sm[j2], i2, banks)
                    for b in range(banks):
                        for g in range(gb):
                            e = (b * gb + g) * P
                            ins = pe.transpose(ps[0:P, bank0 + (j % 2) * banks + b, g * C:(g + 1) * C], hi[:, j, e:e + P], ident[:, :])
                        ins.then_inc(tr[j], 1)

                return slots, [(0, turn)], None

            def vector(dve):
                def add(i, j):
                    wait_use(dve, gx[j], i, 32 if dense else 16)
                    if dense:
                        wait_use(dve, sto[j], i - 1, 32)
                    for b in range(banks):
                        wait_use(dve, tr[j], i, banks, b + 1)
                        part = slice(b * gb, (b + 1) * gb)
                        rows = ot[:, j, part, :] if dense else rows_dst[:, bass.ds((i * slots + j) * groups, groups), :]
                        dve.tensor_tensor(rows, ps[0:P, bank0 + (j % 2) * banks + b, 0:gb * C].rearrange("p (g c) -> p g c", g=gb),
                                          xt[:, j, part, :], ALU.add).then_inc(sm[j], 1)

                return slots, [(0, add)], None

            return dict(sync=sync, gpsimd=gpsimd, scalar=scalar, tensor=tensor, vector=vector)

        with Phase(nc, "norm") as ph:
            ps = ph.pb("ps", 6)
            side_by_side(ph, DI, [layer_norm(ph, "ln_src", QS, QG, src_c, hs[0], (ps, 4, 2), False), map_scatter(ph),
                                  layer_norm(ph, "ln_dense", NS, G, None, h0, (ps, 0, 2), True)])
        fold(0, 1, NT * CH, w1, wfold[1], bias[1], bfold[1], masks=True)
        with Phase(nc, "l1") as ph:
            ps = ph.pb("ps", 6)
            side_by_side(ph, DI, [layer_norm(ph, "ln_dst", QS, QG, dst_c, hd[0], (ps, 4, 2), False, x_dst),
                                  map_gather(ph), dense_layer(ph, 1, 1, 2, h0, h1, ps)])
        source_rows()
        with Phase(nc, "l1_edges") as ph:
            side_by_side(ph, EC // E1S, [edge_layer(ph, 1, ph.pb("ps", 8), E1S)])
        fold(1, 2, BN, wroot[2], wfold[2], bias[2], bfold[2])
        front.close()
        with Phase(nc, "l2") as ph:
            ps = ph.pb("ps", 8)
            splitting, dense = dense_layer(ph, 2, 2, 2, h1, h2, ps)
            side_by_side(ph, DI, [splitting, edge_layer(ph, 2, ps, ES), dense])
        fold(2, 2, BN, wroot[3], wfold[3], bias[3], bfold[3])
        with Phase(nc, "l3") as ph:
            ps = ph.pb("ps", 8)
            side_by_side(ph, DI, [edge_layer(ph, 3, ps, ES), dense_layer(ph, 3, 2, 1, h2, h3, ps)])
        fold(3, 1, BN, None, None, None, None)
        with Phase(nc, "out") as ph:
            ps = ph.pb("ps", 6)
            rows_dst = ph.sb("rows_dst", [P, ET, C])
            dense_stored = ph.slots("od_stored", NS)
            side_by_side(ph, DI, [output(ph, "od", NS, G, 0, ps), output(ph, "oe", QS, QG, 4, ps)])


def kernel(**inputs):
    import numpy as np
    import concourse.bacc as bacc
    from concourse.bass_utils import run_bass_kernel_spmd as run

    nc = bacc.Bacc("TRN2", target_bir_lowering=False, num_devices=1)
    arrays, aps = {}, {}
    for name in inputs:
        a = np.ascontiguousarray(inputs[name])
        arrays["in_" + name] = a
        aps[name] = nc.dram_tensor("in_" + name, a.shape, mybir.dt.from_np(a.dtype), kind="ExternalInput").ap()
    n, e = inputs["x"].shape[0], inputs["src"].shape[0]
    out = nc.dram_tensor("out", (n + e, C), FP, kind="ExternalOutput").ap()
    prm = {name[len("L0_gnn_"):]: aps[name] for name in inputs if name.startswith("L0_gnn_")}
    build(nc, aps["x"], aps["src"], aps["dst"], aps["edge_weight"], prm, out)
    r = run(nc, [arrays], core_ids=[0])
    return r.results[0]["out"][:n]
```
